# Optimizing a Trainium2 kernel written in Bass

```python
import numpy as np
import jax
import jax.numpy as jnp

def _softmax(x, axis=-1):
    return jax.nn.softmax(x, axis=axis)
def _gelu(x):
    return jax.nn.gelu(x, approximate=True)
def _silu(x):
    return jax.nn.silu(x)
def _sigmoid(x):
    return jax.nn.sigmoid(x)
def _layernorm(x, axis=-1, eps=1e-5):
    m = jnp.mean(x, axis=axis, keepdims=True)
    v = jnp.var(x, axis=axis, keepdims=True)
    return (x - m) / jnp.sqrt(v + eps)
def _scatter_add(tgt, idx, src, axis=0):
    return tgt.at[idx].add(src)
def _segment_sum(src, seg, n):
    return jax.ops.segment_sum(src, seg, n)

kernel_name = 'mk_conv_preact_d2_conv_nchw64_3ab5a7'

def setup_inputs(seed: int = 0):
    np.random.seed(seed)
    _w = jnp.asarray
    def _rec_inputs():
        import jax
        import jax.numpy as jnp
        _gk = jax.random.key(seed)
        x = -0.0002091 + 1 * jax.random.normal(jax.random.fold_in(_gk, 1), (32, 64, 112, 112), jnp.float32)
        return x
    x = _rec_inputs()
    def _L0_conv_setup():
        import jax, jax.numpy as jnp
        import numpy as np
        STRIDE = 1
        PADDING = 1
        key = jax.random.key(seed)
        k1, k2 = jax.random.split(key)
        inp = jax.random.normal(k1, (32, 64, 112, 112), dtype=jnp.float32)
        fan_out = 64 * 3 * 3
        weight = jax.random.normal(k2, (64, 64, 3, 3), dtype=jnp.float32) * jnp.sqrt(2.0 / fan_out)
        alpha = jnp.ones((64, 1, 1, 1), dtype=jnp.float32)
        return {'input': inp, 'weight': weight, 'alpha': alpha}
    _L0_conv_all = _L0_conv_setup()
    _L0_conv_in = {k: v for k, v in _L0_conv_all.items() if k in ('weight', 'alpha', )}
    del _L0_conv_all

    def _L1_conv_setup():
        import jax, jax.numpy as jnp
        from jax import lax
        import numpy as np
        B, DIM, HF, H, W, P = (4, 64, 128, 256, 256, 8)
        key = jax.random.key(seed)
        k0, k1, k2, k3, k4 = jax.random.split(key, 5)
        C2 = 2 * HF
        x = jax.random.normal(k0, (B, DIM, H, W), dtype=jnp.float32)
        w_in = jax.random.normal(k1, (C2, DIM), dtype=jnp.float32) * 0.05
        w_dw = jax.random.normal(k2, (C2, 1, 3, 3), dtype=jnp.float32) * 0.1
        fft_filt = 1.0 + 0.1 * jax.random.normal(k3, (C2, 1, 1, P, P // 2 + 1), dtype=jnp.float32)
        w_out = jax.random.normal(k4, (DIM, HF), dtype=jnp.float32) * 0.05
        return {'x': x, 'w_in': w_in, 'w_dw': w_dw, 'fft_filt': fft_filt, 'w_out': w_out}
    _L1_conv_all = _L1_conv_setup()
    _L1_conv_in = {k: v for k, v in _L1_conv_all.items() if k in ('w_in', 'w_dw', 'fft_filt', 'w_out', )}
    del _L1_conv_all

    return {
        "x": x,
        "L0_conv_weight": _L0_conv_in["weight"],
        "L0_conv_alpha": _L0_conv_in["alpha"],
        "L1_conv_w_in": _L1_conv_in["w_in"],
        "L1_conv_w_dw": _L1_conv_in["w_dw"],
        "L1_conv_fft_filt": _L1_conv_in["fft_filt"],
        "L1_conv_w_out": _L1_conv_in["w_out"],
    }

def reference(x, L0_conv_weight, L0_conv_alpha, L1_conv_w_in, L1_conv_w_dw, L1_conv_fft_filt, L1_conv_w_out):
    import jax
    import jax.numpy as jnp
    def _L0_conv_ref(input, weight, alpha):
        import jax, jax.numpy as jnp
        import numpy as np
        STRIDE = 1
        PADDING = 1
        sign = jnp.where(weight >= 0, 1.0, -1.0).astype(weight.dtype)
        binary_weight = sign * alpha
        bw = jax.lax.stop_gradient(binary_weight - weight) + weight
        out = jax.lax.conv_general_dilated(input, bw, window_strides=(STRIDE, STRIDE), padding=((PADDING, PADDING), (PADDING, PADDING)), dimension_numbers=('NCHW', 'OIHW', 'NCHW'))
        return out

    def _L1_conv_ref(x, w_in, w_dw, fft_filt, w_out):
        import jax, jax.numpy as jnp
        from jax import lax
        import numpy as np
        B, DIM, HF, H, W, P = (4, 64, 128, 256, 256, 8)
        h = jnp.einsum('oc,bchw->bohw', w_in, x)
        b, c, hh, ww = h.shape
        hp = h.reshape(b, c, hh // P, P, ww // P, P).transpose(0, 1, 2, 4, 3, 5)
        f = jnp.fft.rfft2(hp.astype(jnp.float32)) * fft_filt
        hp = jnp.fft.irfft2(f, s=(P, P))
        h = hp.transpose(0, 1, 2, 4, 3, 5).reshape(b, c, hh, ww)
        h = lax.conv_general_dilated(h, w_dw, (1, 1), 'SAME', feature_group_count=c, dimension_numbers=('NCHW', 'OIHW', 'NCHW'))
        x1, x2 = jnp.split(h, 2, axis=1)
        g = jax.nn.gelu(x1, approximate=False) * x2
        return jnp.einsum('oc,bchw->bohw', w_out, g)

    def _gn(v, G=32, eps=1e-5):
        B_, C_, H_, W_ = v.shape
        g = v.reshape(B_, G, C_ // G, H_, W_)
        m = jnp.mean(g, axis=(2, 3, 4), keepdims=True)
        s = jnp.var(g, axis=(2, 3, 4), keepdims=True)
        return ((g - m) / jnp.sqrt(s + eps)).reshape(v.shape)

    def _ln_c(v, eps=1e-6):
        m = jnp.mean(v, axis=1, keepdims=True)
        s = jnp.var(v, axis=1, keepdims=True)
        return (v - m) / jnp.sqrt(s + eps)

    def _ln_t(v, eps=1e-5):
        m = jnp.mean(v, axis=-1, keepdims=True)
        s = jnp.var(v, axis=-1, keepdims=True)
        return (v - m) / jnp.sqrt(s + eps)

    def _to_tokens(v):
        B_, C_, H_, W_ = v.shape
        return v.reshape(B_, C_, H_ * W_).transpose(0, 2, 1)
    def _from_tokens(t, like):
        B_, C_, H_, W_ = like.shape
        return t.transpose(0, 2, 1).reshape(B_, C_, H_, W_)

    x = x + _L0_conv_ref(_gn(x), L0_conv_weight, L0_conv_alpha)
    x = x + _L1_conv_ref(_gn(x), L1_conv_w_in, L1_conv_w_dw, L1_conv_fft_filt, L1_conv_w_out)
    return x


_drawn_inputs = setup_inputs


def setup_inputs(seed=0):
    import zlib

    import numpy as np

    out = dict(_drawn_inputs(seed))
    spreads = {'L0_conv_alpha': (1.0, 0.2)}
    factors = {'L1_conv_w_in': 8.0, 'L1_conv_w_dw': 8.0, 'L1_conv_fft_filt': 8.0, 'L1_conv_w_out': 8.0}
    for name, (base, spread) in spreads.items():
        noise = np.random.default_rng([zlib.crc32(name.encode()), seed]).standard_normal(out[name].shape)
        drawn = base * np.exp(spread * noise) if base else spread * noise
        out[name] = jnp.asarray(drawn.astype(out[name].dtype))
    for name, factor in factors.items():
        out[name] = (out[name] * factor).astype(out[name].dtype)
    return out
```

```python
import numpy as np
import concourse.bass as bass
from concourse import mybir
from contextlib import ExitStack

F32 = mybir.dt.float32
F16 = mybir.dt.float16
ACT = mybir.ActivationFunctionType
ALU = mybir.AluOpType
AX = mybir.AxisListType

P = 8
C = 64
C2 = 256
HC = 128
ROWS = P
BW = 2 * P
BPX = P * BW
GN_EPS = 1e-5
RING_STRIPS = 7
PE_TAPS = [(0, 0), (0, -1), (0, 1)]
DVE_TAPS = [(-1, -1), (-1, 0), (-1, 1), (1, -1), (1, 0), (1, 1)]


def patch_basis():
    r, s = np.meshgrid(np.arange(P), np.arange(P), indexing="ij")
    columns, picks = [], []
    for k2 in range(P // 2 + 1):
        edge = k2 in (0, P // 2)
        for k1 in range(P // 2 + 1 if edge else P):
            angle = 2 * np.pi * (k1 * r + k2 * s) / P
            mirror = (-k1) % P if edge else k1
            for wave in (np.cos(angle), np.sin(angle)):
                norm = np.sqrt((wave ** 2).sum())
                if norm > 1e-6:
                    columns.append((wave / norm).reshape(-1))
                    picks.append((k1 * (P // 2 + 1) + k2, mirror * (P // 2 + 1) + k2))
    basis = np.stack(columns, axis=1)
    assert basis.shape == (P * P, P * P) and np.allclose(basis.T @ basis, np.eye(P * P))
    return basis, picks


def shape_constants():
    basis, picks = patch_basis()
    px = [(r * BW + patch * P + s) for patch in range(2) for r in range(P) for s in range(P)]
    forward = np.zeros((BPX, BPX))
    pick = np.zeros((P * (P // 2 + 1), BPX))
    for patch in range(2):
        at = px[patch * P * P:(patch + 1) * P * P]
        forward[np.ix_(at, range(patch * P * P, (patch + 1) * P * P))] = basis
        for f, (a, b) in enumerate(picks):
            pick[a, patch * P * P + f] += 0.5
            pick[b, patch * P * P + f] += 0.5
    pair = np.kron(np.eye(HC // 2), np.full((2, 2), 0.5))
    return {"forward": forward, "inverse": forward.T, "pick": pick, "pair": pair, "identity": np.eye(HC)}


def build(nc, x, conv_w, alpha, w_in, w_dw, filt, w_out, forward, inverse, pick, pair, identity, out):
    B, _, H, W = x.shape
    STRIPS = H // ROWS
    NBLK = W // BW
    NPX = ROWS * W
    TILE = NPX // 2
    PITCH = W + 2
    RING = RING_STRIPS * ROWS
    NF = P * (P // 2 + 1)
    IMG = H * W

    ctx = ExitStack()
    with ctx:
        def sb(name, shape, dt=F32):
            return ctx.enter_context(nc.sbuf_tensor(name, shape, dt))

        def sem(name):
            return ctx.enter_context(nc.semaphore(name))

        c_fwd = sb("c_fwd", [BPX, BPX])
        c_inv = sb("c_inv", [BPX, BPX])
        c_pick = sb("c_pick", [NF, BPX])
        c_pair = sb("c_pair", [128, 128])
        c_id = sb("c_id", [128, 128])
        alpha_sb = sb("alpha_sb", [128, 1])
        win_sb = sb("win_sb", [C, C2])
        wdw_sb = sb("wdw_sb", [HC, 2, 9])
        filt_sb = sb("filt_sb", [NF, C2])
        wout_sb = sb("wout_sb", [HC, C])
        craw = sb("craw", [128, 9, C])
        cge = sb("cge", [128, 9, C])
        csign = sb("csign", [128, 4, 3, 128], F16)
        mult = sb("mult", [BPX, C2])
        diag = sb("diag", [HC, 2, len(PE_TAPS), HC])

        X = sb("X", [128, H, W])
        S = sb("S", [128, H + 2, PITCH], F16)
        n32 = sb("n32", [128, 2, ROWS, W])
        junk = sb("junk", [128, NPX])
        sums = sb("sums", [128, 2, STRIPS])
        statx = sb("statx", [128, 2])
        ngmx = sb("ngmx", [128, 1])
        varx = sb("varx", [128, 1])
        vex = sb("vex", [128, 1])
        rstdx = sb("rstdx", [128, 1])
        nbx = sb("nbx", [128, 1])
        bn = sb("bn", [C, 2 * STRIPS, 6])
        mv = sb("mv", [128, 2])
        dev = sb("dev", [128, 1])
        m_half = sb("m_half", [128, 1])
        spread = sb("spread", [128, 1])
        gm1 = sb("gm1", [128, 1])
        ve1 = sb("ve1", [128, 1])
        rstd1 = sb("rstd1", [128, 1])
        nb1 = sb("nb1", [128, 1])

        xn = sb("xn", [128, NBLK, ROWS, BW])
        xT = sb("xT", [BPX, NBLK, C])
        xf = sb("xf", [C, NBLK, BPX])
        hf = sb("hf", [BPX, NBLK, C2])
        h = sb("h", [HC, 2, RING, PITCH])
        gel = sb("gel", [HC, NPX])
        g = sb("g", [HC, NPX])
        o = sb("o", [C, 2, NPX])

        PS = ctx.enter_context(nc.psum_tensor("PS", [128, 8, 512], F32))
        bank = [PS[:, i, :] for i in range(8)]

        def banks(a, n, m=128):
            return PS[0:m, a:a + 2, :].rearrange("p a b -> p (a b)")[:, 0:n]

        dma_const = sem("dma_const")
        dma_conv = sem("dma_conv")
        dma_x = sem("dma_x")
        dma_out = [sem("dma_out0"), sem("dma_out1")]
        pool_zero = sem("pool_zero")
        pool_lo = sem("pool_lo")
        pool_rstdx = sem("pool_rstdx")
        pool_rstd1 = sem("pool_rstd1")
        dve_prep = sem("dve_prep")
        dve_csign = sem("dve_csign")
        dve_sq = sem("dve_sq")
        pe_mult = sem("pe_mult")
        pe_statx = sem("pe_statx")
        pe_stat1 = sem("pe_stat1")
        pe_conv = sem("pe_conv")
        pe_xT = sem("pe_xT")
        pe_xf = sem("pe_xf")
        pe_hf = sem("pe_hf")
        pe_h = sem("pe_h")
        pe_dwA = sem("pe_dwA")
        pe_dwB = sem("pe_dwB")
        pe_out = sem("pe_out")
        act_sum = sem("act_sum")
        act_statx = sem("act_statx")
        act_n32 = sem("act_n32")
        act_hi = sem("act_hi")
        act_xn = sem("act_xn")
        act_xT = sem("act_xT")
        act_xf = sem("act_xf")
        act_h = sem("act_h")
        act_gel = sem("act_gel")
        dve_statx = sem("dve_statx")
        dve_conv = sem("dve_conv")
        dve_bn = sem("dve_bn")
        dve_stat1 = sem("dve_stat1")
        dve_tap = sem("dve_tap")
        dve_hf = sem("dve_hf")
        dve_g = sem("dve_g")
        dve_o = sem("dve_o")
        N_CONST = 10

        def tap_pieces(s, dy):
            rows = [i for i in range(ROWS) if 0 <= s * ROWS + i + dy < H]
            cuts = [i for i in rows[1:] if (s * ROWS + i + dy) % RING == 0]
            if len(rows) == ROWS and not cuts:
                return [(0, ROWS)]
            edges = sorted({rows[0], rows[-1] + 1, *cuts, *([ROWS // 2] if rows[0] < ROWS // 2 < rows[-1] + 1 else [])})
            return list(zip(edges[:-1], edges[1:]))

        TAP_OPS = [sum(len(tap_pieces(s, dy)) for dy, _ in DVE_TAPS) for s in range(STRIPS)]
        TAPS_IMG = 2 * sum(TAP_OPS)

        def tap_base(s, half):
            return 2 * sum(TAP_OPS[:s]) + (TAP_OPS[s] if half else 0)

        SUM_STEPS = {2 + j // 4: [] for j in range(STRIPS)}
        for j in range(STRIPS):
            SUM_STEPS[2 + j // 4].append(j)
        SQ_STEPS = {6: [], 7: [], 8: []}
        for j in range(STRIPS):
            SQ_STEPS[6 + j // 5].append(j)
        NORM_STEPS = {9: [], 10: [], 11: [], 12: [], 13: []}
        for j in range(STRIPS):
            NORM_STEPS[9 + j // 3].append(j)
        MEAN_STEP, VAR_STEP = 5, 8
        STEPS = STRIPS + 3

        block = ctx.enter_context(nc.Block())

        @block.sync
        def _(sp):
            for dst, src in ((c_fwd, forward), (c_inv, inverse), (c_pick, pick), (c_pair, pair), (c_id, identity),
                             (win_sb, w_in), (filt_sb, filt), (wout_sb, w_out)):
                sp.dma_start(dst[:], src).then_inc(dma_const, 16)
            sp.dma_start(wdw_sb[:], w_dw.rearrange("(a c) t -> c a t", a=2)).then_inc(dma_const, 16)
            sp.dma_start(alpha_sb[0:C], alpha).then_inc(dma_const, 16)
            sp.dma_start(X[C:128].rearrange("p a b -> p (a b)"), x[0].rearrange("c a b -> c (a b)")).then_inc(dma_x, 16)
            sp.dma_start(craw[0:C], conv_w).then_inc(dma_conv, 16)
            sp.dma_start(craw[C:128], conv_w).then_inc(dma_conv, 16)
            sp.dma_start(alpha_sb[C:128], alpha).then_inc(dma_conv, 16)

            def image(b, first, more):
                if more:
                    sp.wait_ge(dve_conv, b * 2 * STRIPS + 2 * STRIPS)
                    sp.dma_start(X[C:128].rearrange("p a b -> p (a b)"),
                                 x[b + 1].rearrange("c a b -> c (a b)")).then_inc(dma_x, 16)
                for s in range(STRIPS):
                    sp.wait_ge(dve_o, b * STRIPS + s + 1)
                    sp.dma_start(out[b, :, s * ROWS:(s + 1) * ROWS, :].rearrange("c a b -> c (a b)"),
                                 o[:, s % 2, :]).then_inc(dma_out[s % 2], 16)

            image(0, True, True)
            with sp.Fori(1, B - 1) as b:
                image(b, False, True)
            image(B - 1, False, False)
            sp.wait_ge(dma_out[0], B * 16 * ((STRIPS + 1) // 2))
            sp.wait_ge(dma_out[1], B * 16 * (STRIPS // 2))

        @block.gpsimd
        def _(pool):
            nc.gpsimd.memset(S[:], 0.0).then_inc(pool_zero, 1)
            nc.gpsimd.memset(h[:], 0.0).then_inc(pool_zero, 1)
            nc.gpsimd.memset(statx[:], 0.0).then_inc(pool_zero, 1)
            nc.gpsimd.memset(xn[:], 0.0).then_inc(pool_zero, 1)
            nc.gpsimd.memset(spread[:], 0.0).then_inc(pool_zero, 1)
            nc.gpsimd.memset(csign[:], 0.0).then_inc(pool_zero, 1)
            nc.gpsimd.memset(m_half[:], -0.5).then_inc(pool_zero, 1)
            pool.wait_ge(pool_zero, 7)

            def rstd_x(b):
                pool.wait_ge(dve_statx, b * 4 + 3)
                nc.gpsimd.tensor_tensor(rstdx[:], vex[:], m_half[:], ALU.pow).then_inc(pool_rstdx, 1)

            def rstd_1(b):
                pool.wait_ge(dve_stat1, b * 6 + 5)
                nc.gpsimd.tensor_tensor(rstd1[:], ve1[:], m_half[:], ALU.pow).then_inc(pool_rstd1, 1)

            def low_parts(b):
                for j in range(STRIPS):
                    pool.wait_ge(act_hi, b * STRIPS + j + 1)
                    rows = S[C:128, 1 + j * ROWS:1 + (j + 1) * ROWS, 1:1 + W]
                    nc.gpsimd.tensor_tensor(rows, n32[C:128, j % 2], rows, ALU.subtract).then_inc(pool_lo, 1)

            rstd_x(0)
            low_parts(0)
            with pool.Fori(0, B - 1) as b:
                rstd_1(b)
                rstd_x(b + 1)
                low_parts(b + 1)
            rstd_1(B - 1)

        @block.scalar
        def _(act):
            def sum_strip(b, j):
                if j == 0:
                    act.wait_ge(dma_x, b * 16 + 16)
                nc.scalar.activation(junk[C:128], X[C:128, j * ROWS:(j + 1) * ROWS, :].rearrange("p a b -> p (a b)"),
                                     ACT.Copy, accum_out=sums[C:128, 0, j:j + 1]).then_inc(act_sum, 1)
                act.wait_ge(act_sum, b * 2 * STRIPS + j + 1)

            def square_strip(b, j):
                if j == 0:
                    act.wait_ge(act_statx, b * 2 + 1)
                nc.scalar.activation(junk[C:128], X[C:128, j * ROWS:(j + 1) * ROWS, :].rearrange("p a b -> p (a b)"),
                                     ACT.Square, bias=ngmx[C:128], accum_out=sums[C:128, 1, j:j + 1]).then_inc(act_sum, 1)
                act.wait_ge(act_sum, b * 2 * STRIPS + STRIPS + j + 1)

            def mean_to_sbuf(b):
                act.wait_ge(pe_statx, b * 2 + 1)
                nc.scalar.mul(ngmx[:], bank[5][:, 0:1], -1.0 / IMG).then_inc(act_statx, 1)

            def variance_to_sbuf(b):
                act.wait_ge(pe_statx, b * 2 + 2)
                nc.scalar.mul(varx[:], bank[5][:, 0:1], 1.0 / IMG).then_inc(act_statx, 1)

            def normalise_strip(b, first, j):
                if j == 0:
                    act.wait_ge(dve_statx, b * 4 + 4)
                if j >= 2:
                    act.wait_ge(pool_lo, b * STRIPS + j - 1)
                elif not first:
                    act.wait_ge(pool_lo, b * STRIPS + j)
                nc.scalar.activation(n32[C:128, j % 2], X[C:128, j * ROWS:(j + 1) * ROWS, :], ACT.Identity,
                                     bias=nbx[C:128], scale=rstdx[C:128]).then_inc(act_n32, 1)
                act.wait_ge(act_n32, b * STRIPS + j + 1)
                nc.scalar.activation(S[0:C, 1 + j * ROWS:1 + (j + 1) * ROWS, 1:1 + W], n32[C:128, j % 2], ACT.Copy)
                nc.scalar.activation(S[C:128, 1 + j * ROWS:1 + (j + 1) * ROWS, 1:1 + W], n32[C:128, j % 2],
                                     ACT.Copy).then_inc(act_hi, 1)

            def image(b, first, more):
                for t in range(STEPS):
                    n, i, s = t, t - 1, t - 2
                    if n == 0:
                        act.wait_ge(dve_stat1, b * 6 + 6)

                        def normalise_x1(m):
                            if m >= 1:
                                act.wait_ge(pe_xT, b * STRIPS + m)
                            nc.scalar.activation(xn[0:C].rearrange("p k r c -> p r k c"),
                                                 X[0:C, m * ROWS:(m + 1) * ROWS, :].rearrange("p r (k c) -> p r k c", c=BW),
                                                 ACT.Identity, bias=nb1[0:C], scale=rstd1[0:C]).then_inc(act_xn, 1)
                        normalise_x1(0)
                    if 0 <= i < STRIPS:
                        ring = (i * ROWS) % RING
                        for half in range(2):
                            act.wait_ge(pe_h, b * 2 * STRIPS + 2 * i + half + 1)
                            if half == 0:
                                if i >= RING_STRIPS - 1:
                                    act.wait_ge(dve_tap, b * TAPS_IMG + tap_base(i - RING_STRIPS + 2, 0))
                                elif not first:
                                    act.wait_ge(dve_tap, b * TAPS_IMG)
                            nc.scalar.activation(
                                h[:, half, ring:ring + ROWS, 1:1 + W].rearrange("p r (k c) -> p k r c", c=BW),
                                banks(4 + 2 * half, NBLK * BPX).rearrange("p (k r c) -> p k r c", k=NBLK, r=ROWS),
                                ACT.Copy).then_inc(act_h, 1)
                    if n < STRIPS:
                        act.wait_ge(pe_xT, b * STRIPS + n + 1)
                        if n >= 1:
                            act.wait_ge(pe_xf, b * STRIPS + n)
                        nc.scalar.activation(xT[:].rearrange("p k c -> p (k c)"), bank[4][:, 0:NBLK * C],
                                             ACT.Copy).then_inc(act_xT, 1)
                    if more and t == MEAN_STEP + 1:
                        mean_to_sbuf(b + 1)
                    if more and t == VAR_STEP + 1:
                        variance_to_sbuf(b + 1)
                    if n < STRIPS:
                        act.wait_ge(pe_xf, b * STRIPS + n + 1)
                        if n >= 1:
                            act.wait_ge(pe_hf, b * 2 * STRIPS + 2 * n)
                        nc.scalar.activation(xf[:].rearrange("p k f -> p (k f)"), banks(4, NBLK * BPX, C),
                                             ACT.Copy).then_inc(act_xf, 1)
                        if n + 1 < STRIPS:
                            normalise_x1(n + 1)
                    if 0 <= s < STRIPS:
                        act.wait_ge(dve_tap, b * TAPS_IMG + tap_base(s, 1))
                        if s or not first:
                            act.wait_ge(dve_g, b * STRIPS + s)
                        nc.scalar.activation(gel[:].rearrange("p (a b) -> p a b", a=2), PS[:, 0:2, 0:TILE],
                                             ACT.Gelu).then_inc(act_gel, 1)
                    if more:
                        for j in SUM_STEPS.get(t, ()):
                            sum_strip(b + 1, j)
                        for j in SQ_STEPS.get(t, ()):
                            square_strip(b + 1, j)
                        for j in NORM_STEPS.get(t, ()):
                            normalise_strip(b + 1, False, j)

            for j in range(STRIPS):
                sum_strip(0, j)
            mean_to_sbuf(0)
            for j in range(STRIPS):
                square_strip(0, j)
            variance_to_sbuf(0)
            act.wait_ge(pool_zero, 1)
            for j in range(STRIPS):
                normalise_strip(0, True, j)
            image(0, True, True)
            with act.Fori(1, B - 1) as b:
                image(b, False, True)
            image(B - 1, False, False)

        @block.vector
        def _(dve):
            dve.wait_ge(dma_conv, 48)
            nc.vector.tensor_scalar(cge[:], craw[:], 0.0, 2.0, ALU.is_ge, ALU.mult).then_inc(dve_sq, 1)
            dve.wait_ge(dve_sq, 1)
            dve.wait_ge(pool_zero, 6)
            for d in range(4):
                for odd in range(2):
                    ky = d - odd
                    if 0 <= ky < 3:
                        nc.vector.tensor_scalar(csign[:, d, :, odd * C:(odd + 1) * C], cge[:, 3 * ky:3 * ky + 3, :],
                                                1.0, None, ALU.subtract).then_inc(dve_csign, 1)
            dve.wait_ge(dma_const, 16 * N_CONST)
            for half in range(2):
                for k, (dy, dx) in enumerate(PE_TAPS):
                    at = (dy + 1) * 3 + dx + 1
                    nc.vector.tensor_scalar(diag[:, half, k, :], c_id[:], wdw_sb[:, half, at:at + 1], None,
                                            ALU.mult).then_inc(dve_prep, 1)
            dve.wait_ge(pe_mult, 1)
            nc.vector.tensor_copy(mult[:], bank[7][:, 0:C2]).then_inc(dve_prep, 1)

            def sum_statx(b):
                dve.wait_ge(act_sum, b * 2 * STRIPS + STRIPS)
                nc.vector.reduce_sum(statx[C:128, 0:1], sums[C:128, 0, :], axis=AX.X).then_inc(dve_statx, 1)

            def square_statx(b):
                dve.wait_ge(act_sum, b * 2 * STRIPS + 2 * STRIPS)
                nc.vector.reduce_sum(statx[C:128, 1:2], sums[C:128, 1, :], axis=AX.X).then_inc(dve_statx, 1)

            def scale_statx(b):
                dve.wait_ge(act_statx, b * 2 + 2)
                nc.vector.tensor_scalar(vex[:], varx[:], GN_EPS, None, ALU.add).then_inc(dve_statx, 1)
                dve.wait_ge(pool_rstdx, b + 1)
                nc.vector.tensor_tensor(nbx[:], ngmx[:], rstdx[:], ALU.mult).then_inc(dve_statx, 1)

            def taps(b, s, half, which):
                base = b * TAPS_IMG + tap_base(s, half)
                k = 0
                for n, (dy, dx) in enumerate(DVE_TAPS):
                    at = (dy + 1) * 3 + dx + 1
                    for i0, i1 in tap_pieces(s, dy):
                        k += 1
                        if n not in which:
                            continue
                        if k > 1:
                            dve.wait_ge(dve_tap, base + k - 1)
                        elif half == 0:
                            dve.wait_ge(pe_dwA, b * STRIPS + s + 1)
                        else:
                            dve.wait_ge(pe_dwB, b * STRIPS + s + 1)
                        if dy == 1 and dx == -1:
                            dve.wait_ge(act_h, b * 2 * STRIPS + 2 * min(s + 1, STRIPS - 1) + half + 1)
                        row = (s * ROWS + i0 + dy) % RING
                        src = h[:, half, row:row + i1 - i0, 1 + dx:1 + dx + W]
                        if i1 - i0 == ROWS:
                            acc = PS[:, 2 * half:2 * half + 2, 0:TILE].rearrange("p a (r c) -> p a r c", c=W)
                            src = src.rearrange("p (a r) c -> p a r c", a=2)
                        else:
                            q = i0 // (ROWS // 2)
                            acc = bank[2 * half + q][:, (i0 - q * (ROWS // 2)) * W:(i1 - q * (ROWS // 2)) * W]
                            acc = acc.rearrange("p (r c) -> p r c", c=W)
                        nc.vector.scalar_tensor_tensor(out=acc, in0=src, scalar=wdw_sb[:, half, at:at + 1], in1=acc,
                                                       op0=ALU.mult, op1=ALU.add).then_inc(dve_tap, 1)

            def image(b, first, more):
                for j in range(STRIPS):
                    dve.wait_ge(pe_conv, b * STRIPS + j + 1)
                    if j == 0 and not first:
                        dve.wait_ge(act_xn, b * STRIPS)
                    for odd in range(2):
                        rows = slice(j * ROWS + odd, (j + 1) * ROWS, 2)
                        nc.vector.scalar_tensor_tensor(
                            out=X[0:C, rows, :],
                            in0=bank[4 + j % 4][odd * C:(odd + 1) * C, 0:TILE].rearrange("p (r c) -> p r c", c=W),
                            scalar=alpha_sb[odd * C:(odd + 1) * C], in1=X[C:128, rows, :],
                            op0=ALU.mult, op1=ALU.add).then_inc(dve_conv, 1)
                    dve.wait_ge(dve_conv, b * 2 * STRIPS + 2 * j + 2)
                    for k in range(2):
                        row0 = j * ROWS + k * ROWS // 2
                        nc.vector.bn_stats(bn[:, 2 * j + k, :],
                                           X[0:C, row0:row0 + ROWS // 2, :].rearrange("p a b -> p (a b)")).then_inc(dve_bn, 1)
                dve.wait_ge(dve_bn, b * 2 * STRIPS + 2 * STRIPS)
                nc.vector.memset(mv[C:128], 0.0)
                nc.vector.bn_aggr(mv[0:C], bn[:].rearrange("p a b -> p (a b)")).then_inc(dve_stat1, 1)
                dve.wait_ge(pe_stat1, b * 2 + 1)
                dve.wait_ge(dve_stat1, b * 6 + 1)
                nc.vector.tensor_tensor(dev[:], mv[:, 0:1], bank[5][:, 0:1], ALU.subtract).then_inc(dve_stat1, 1)
                nc.vector.tensor_copy(gm1[:], bank[5][:, 0:1]).then_inc(dve_stat1, 1)
                dve.wait_ge(dve_stat1, b * 6 + 3)
                nc.vector.scalar_tensor_tensor(out=spread[0:C], in0=dev[0:C], scalar=dev[0:C], in1=mv[0:C, 1:2],
                                               op0=ALU.mult, op1=ALU.add).then_inc(dve_stat1, 1)
                dve.wait_ge(pe_stat1, b * 2 + 2)
                nc.vector.tensor_scalar(ve1[:], bank[6][:, 0:1], GN_EPS, None, ALU.add).then_inc(dve_stat1, 1)
                dve.wait_ge(pool_rstd1, b + 1)
                nc.vector.scalar_tensor_tensor(out=nb1[:], in0=gm1[:], scalar=-1.0, in1=rstd1[:],
                                               op0=ALU.mult, op1=ALU.mult).then_inc(dve_stat1, 1)

                for t in range(STEPS):
                    n, s, w = t, t - 2, t - 3
                    if 0 <= s < STRIPS:
                        taps(b, s, 0, range(0, 6))
                    if 0 <= w < STRIPS:
                        dve.wait_ge(pe_out, b * STRIPS + w + 1)
                        if w >= 2:
                            dve.wait_ge(dma_out[w % 2], b * 16 * (STRIPS // 2) + 16 * (w // 2))
                        elif not first:
                            dve.wait_ge(dma_out[w % 2], b * 16 * (STRIPS // 2))
                        nc.vector.tensor_tensor(
                            o[:, w % 2, :].rearrange("p (a b) -> p a b", a=2), PS[0:C, 6:8, 0:TILE],
                            X[0:C, w * ROWS:(w + 1) * ROWS, :].rearrange("p (a r) c -> p a (r c)", a=2),
                            ALU.add).then_inc(dve_o, 1)
                    if 0 <= s < STRIPS:
                        taps(b, s, 1, range(0, 3))
                    if n < STRIPS:
                        if n or not first:
                            dve.wait_ge(pe_h, b * 2 * STRIPS + 2 * n)
                        for part, (at, k0, k1) in enumerate(((6, 0, 4), (4, 4, NBLK))):
                            dve.wait_ge(pe_hf, b * 2 * STRIPS + 2 * n + part + 1)
                            nc.vector.tensor_tensor(
                                hf[:, k0:k1, :], banks(at, (k1 - k0) * C2).rearrange("p (k c) -> p k c", c=C2),
                                mult[:].unsqueeze(1).broadcast_to([BPX, k1 - k0, C2]), ALU.mult).then_inc(dve_hf, 1)
                    if 0 <= s < STRIPS:
                        taps(b, s, 1, range(3, 6))
                        dve.wait_ge(dve_tap, b * TAPS_IMG + tap_base(s + 1, 0))
                        dve.wait_ge(act_gel, b * STRIPS + s + 1)
                        if s or not first:
                            dve.wait_ge(pe_out, b * STRIPS + s)
                        nc.vector.tensor_tensor(g[:].rearrange("p (a b) -> p a b", a=2),
                                                gel[:].rearrange("p (a b) -> p a b", a=2), PS[:, 2:4, 0:TILE],
                                                ALU.mult).then_inc(dve_g, 1)
                    if more and t == MEAN_STEP:
                        sum_statx(b + 1)
                    if more and t == VAR_STEP:
                        square_statx(b + 1)
                    if more and t == VAR_STEP + 1:
                        scale_statx(b + 1)

            dve.wait_ge(pool_zero, 6)
            sum_statx(0)
            square_statx(0)
            scale_statx(0)
            image(0, True, True)
            with dve.Fori(1, B - 1) as b:
                image(b, False, True)
            image(B - 1, False, False)

        @block.tensor
        def _(pe):
            def mean_x(b):
                pe.wait_ge(dve_statx, b * 4 + 1)
                nc.tensor.matmul(bank[5][:, 0:1], c_pair[:], statx[:, 0:1], start=True, stop=True).then_inc(pe_statx, 1)

            def variance_x(b):
                pe.wait_ge(dve_statx, b * 4 + 2)
                nc.tensor.matmul(bank[5][:, 0:1], c_pair[:], statx[:, 1:2], start=True, stop=True).then_inc(pe_statx, 1)

            pe.wait_ge(dma_const, 16 * N_CONST)
            nc.tensor.matmul(bank[7][:, 0:C2], c_pick[:], filt_sb[:], start=True, stop=True).then_inc(pe_mult, 1)
            pe.wait_ge(pool_zero, 6)
            mean_x(0)
            pe.wait_ge(act_statx, 1)
            variance_x(0)
            pe.wait_ge(dve_prep, 2 * len(PE_TAPS) + 1)
            pe.wait_ge(dve_csign, 6)
            pe.wait_ge(act_statx, 2)

            def depthwise(b, s, half):
                row = (s * ROWS) % RING
                for q in range(2):
                    for k, (dy, dx) in enumerate(PE_TAPS):
                        r0 = row + q * ROWS // 2
                        last = nc.tensor.matmul(bank[2 * half + q][:, 0:TILE], diag[:, half, k, :],
                                                h[:, half, r0:r0 + ROWS // 2, 1 + dx:1 + dx + W],
                                                start=(k == 0), stop=(k == len(PE_TAPS) - 1))
                last.then_inc(pe_dwA if half == 0 else pe_dwB, 1)

            def image(b, first, more):
                pe.wait_ge(pool_lo, b * STRIPS + STRIPS)
                if not first:
                    pe.wait_ge(dve_o, b * STRIPS)
                for j in range(STRIPS):
                    if j >= 4:
                        pe.wait_ge(dve_conv, b * 2 * STRIPS + 2 * (j - 3))
                    for d in range(4):
                        for kx in range(3):
                            row0 = j * ROWS + d
                            last = nc.tensor.matmul(bank[4 + j % 4][:, 0:TILE], csign[:, d, kx, :],
                                                    S[:, row0:row0 + ROWS - 1:2, kx:kx + W],
                                                    start=(d == 0 and kx == 0), stop=(d == 3 and kx == 2))
                    last.then_inc(pe_conv, 1)
                pe.wait_ge(dve_stat1, b * 6 + 1)
                nc.tensor.matmul(bank[5][:, 0:1], c_pair[:], mv[:, 0:1], start=True, stop=True).then_inc(pe_stat1, 1)
                pe.wait_ge(dve_stat1, b * 6 + 4)
                nc.tensor.matmul(bank[6][:, 0:1], c_pair[:], spread[:], start=True, stop=True).then_inc(pe_stat1, 1)
                pe.wait_ge(dve_stat1, b * 6 + 6)

                for t in range(STEPS):
                    n, i, s, w = t, t - 1, t - 2, t - 3
                    if 0 <= s < STRIPS:
                        pe.wait_ge(act_h, b * 2 * STRIPS + 2 * s + 2)
                        if s or not first:
                            pe.wait_ge(act_gel, b * STRIPS + s)
                        depthwise(b, s, 0)
                    if 0 <= i < STRIPS:
                        pe.wait_ge(dve_hf, b * 2 * STRIPS + 2 * i + 2)
                        for half in range(2):
                            for k in range(NBLK):
                                last = nc.tensor.matmul(banks(4 + 2 * half, NBLK * BPX)[:, k * BPX:(k + 1) * BPX],
                                                        hf[:, k, half * HC:(half + 1) * HC], c_inv[:],
                                                        start=True, stop=True)
                            last.then_inc(pe_h, 1)
                    if n < STRIPS:
                        if i >= 0:
                            pe.wait_ge(act_h, b * 2 * STRIPS + 2 * i + 1)
                        if more and t == MEAN_STEP + 1:
                            mean_x(b + 1)
                        if more and t == VAR_STEP + 1:
                            variance_x(b + 1)
                        pe.wait_ge(act_xn, b * STRIPS + n + 1)
                        nc.tensor.transpose(bank[4][:, (NBLK - 1) * C:(NBLK + 1) * C],
                                            xn[:, NBLK - 1].rearrange("p r c -> p (r c)"), c_id[:])
                        for k in range(NBLK - 1):
                            last = nc.tensor.transpose(bank[4][:, k * C:(k + 1) * C],
                                                       xn[0:C, k].rearrange("p r c -> p (r c)"), c_id[0:C, 0:C])
                        last.then_inc(pe_xT, 1)
                    if 0 <= w < STRIPS:
                        pe.wait_ge(dve_g, b * STRIPS + w + 1)
                        if i < STRIPS:
                            pe.wait_ge(act_h, b * 2 * STRIPS + 2 * i + 2)
                        if w >= 1:
                            pe.wait_ge(dve_o, b * STRIPS + w)
                        for q in range(2):
                            last = nc.tensor.matmul(bank[6 + q][0:C, 0:TILE], wout_sb[:], g[:, q * TILE:(q + 1) * TILE],
                                                    start=True, stop=True)
                        last.then_inc(pe_out, 1)
                    if n < STRIPS:
                        pe.wait_ge(act_xT, b * STRIPS + n + 1)
                        if more and t in (MEAN_STEP + 1, VAR_STEP + 1):
                            pe.wait_ge(act_statx, (b + 1) * 2 + (1 if t == MEAN_STEP + 1 else 2))
                        if i >= 0:
                            pe.wait_ge(act_h, b * 2 * STRIPS + 2 * i + 1)
                        for k in range(NBLK):
                            last = nc.tensor.matmul(banks(4, NBLK * BPX, C)[:, k * BPX:(k + 1) * BPX], xT[:, k, :],
                                                    c_fwd[:], start=True, stop=True)
                        last.then_inc(pe_xf, 1)
                    if 0 <= s < STRIPS:
                        if s or not first:
                            pe.wait_ge(dve_g, b * STRIPS + s)
                        depthwise(b, s, 1)
                    if n < STRIPS:
                        pe.wait_ge(act_xf, b * STRIPS + n + 1)
                        if 0 <= w:
                            pe.wait_ge(dve_o, b * STRIPS + w + 1)
                        if i >= 0:
                            pe.wait_ge(act_h, b * 2 * STRIPS + 2 * i + 2)
                        for at, k0, k1 in ((6, 0, 4), (4, 4, NBLK)):
                            for k in range(k0, k1):
                                last = nc.tensor.matmul(banks(at, (k1 - k0) * C2)[:, (k - k0) * C2:(k - k0 + 1) * C2],
                                                        xf[:, k, :], win_sb[:], start=True, stop=True)
                            last.then_inc(pe_hf, 1)

            image(0, True, True)
            with pe.Fori(1, B - 1) as b:
                image(b, False, True)
            image(B - 1, False, False)


def kernel(x, L0_conv_weight, L0_conv_alpha, L1_conv_w_in, L1_conv_w_dw, L1_conv_fft_filt, L1_conv_w_out):
    import concourse.bacc as bacc
    from concourse.bass_utils import run_bass_kernel_spmd

    nc = bacc.Bacc("TRN2", target_bir_lowering=False, num_devices=1)
    arrays = {
        "x": np.ascontiguousarray(x),
        "conv_w": np.ascontiguousarray(np.transpose(np.asarray(L0_conv_weight), (1, 2, 3, 0))).reshape(C, 9, C),
        "alpha": np.ascontiguousarray(L0_conv_alpha).reshape(C, 1),
        "w_in": np.ascontiguousarray(np.transpose(np.asarray(L1_conv_w_in))),
        "w_dw": np.ascontiguousarray(L1_conv_w_dw).reshape(C2, 9),
        "filt": np.ascontiguousarray(np.transpose(np.asarray(L1_conv_fft_filt).reshape(C2, P * (P // 2 + 1)))),
        "w_out": np.ascontiguousarray(np.transpose(np.asarray(L1_conv_w_out))),
    }
    for name, a in shape_constants().items():
        arrays[name] = np.ascontiguousarray(a, dtype=np.float32)
    aps = {name: nc.dram_tensor(f"in_{name}", a.shape, F32, kind="ExternalInput").ap() for name, a in arrays.items()}
    out = nc.dram_tensor("out_x", arrays["x"].shape, F32, kind="ExternalOutput").ap()
    build(nc, *aps.values(), out)
    ran = run_bass_kernel_spmd(nc, [{f"in_{name}": a for name, a in arrays.items()}], core_ids=[0])
    return ran.results[0]["out_x"]
```

```python
import numpy as np
import concourse.bass as bass
from concourse import mybir
from contextlib import ExitStack

F32 = mybir.dt.float32
F16 = mybir.dt.float16
ACT = mybir.ActivationFunctionType
ALU = mybir.AluOpType
AX = mybir.AxisListType

P = 8
C = 64
C2 = 256
HC = 128
ROWS = P
BW = 2 * P
BPX = P * BW
GN_EPS = 1e-5
RING_STRIPS = 4
ALL_TAPS = [(dy, dx) for dy in (-1, 0, 1) for dx in (-1, 0, 1)]
PE_TAPS = [[(0, 0), (0, -1), (0, 1), (-1, 0)], [(0, 0), (0, -1), (0, 1)]]
DVE_TAPS = [[tap for tap in ALL_TAPS if tap not in taps] for taps in PE_TAPS]


def patch_basis():
    r, s = np.meshgrid(np.arange(P), np.arange(P), indexing="ij")
    columns, picks = [], []
    for k2 in range(P // 2 + 1):
        edge = k2 in (0, P // 2)
        for k1 in range(P // 2 + 1 if edge else P):
            angle = 2 * np.pi * (k1 * r + k2 * s) / P
            mirror = (-k1) % P if edge else k1
            for wave in (np.cos(angle), np.sin(angle)):
                norm = np.sqrt((wave ** 2).sum())
                if norm > 1e-6:
                    columns.append((wave / norm).reshape(-1))
                    picks.append((k1 * (P // 2 + 1) + k2, mirror * (P // 2 + 1) + k2))
    basis = np.stack(columns, axis=1)
    assert basis.shape == (P * P, P * P) and np.allclose(basis.T @ basis, np.eye(P * P))
    return basis, picks


def shape_constants():
    basis, picks = patch_basis()
    px = [(r * BW + patch * P + s) for patch in range(2) for r in range(P) for s in range(P)]
    forward = np.zeros((BPX, BPX))
    pick = np.zeros((P * (P // 2 + 1), BPX))
    for patch in range(2):
        at = px[patch * P * P:(patch + 1) * P * P]
        forward[np.ix_(at, range(patch * P * P, (patch + 1) * P * P))] = basis
        for f, (a, b) in enumerate(picks):
            pick[a, patch * P * P + f] += 0.5
            pick[b, patch * P * P + f] += 0.5
    pair = np.kron(np.eye(HC // 2), np.full((2, 2), 0.5))
    return {"forward": forward, "inverse": forward.T, "pick": pick, "pair": pair, "identity": np.eye(HC)}


def build(nc, x, conv_w, alpha, w_in, w_dw, filt, w_out, forward, inverse, pick, pair, identity, out):
    B, _, H, W = x.shape
    STRIPS = H // ROWS
    NBLK = W // BW
    NPX = ROWS * W
    TILE = NPX // 2
    HALF_ROWS = ROWS // 2
    PITCH = W + 2
    RING = RING_STRIPS * ROWS
    NF = P * (P // 2 + 1)
    IMG = H * W
    assert B % 2 == 0 and (2 * STRIPS) % RING_STRIPS == 0

    ctx = ExitStack()
    with ctx:
        def sb(name, shape, dt=F32):
            return ctx.enter_context(nc.sbuf_tensor(name, shape, dt))

        def sem(name):
            return ctx.enter_context(nc.semaphore(name))

        c_fwd = sb("c_fwd", [BPX, BPX])
        c_inv = sb("c_inv", [BPX, BPX])
        c_pick = sb("c_pick", [NF, BPX])
        c_pair = sb("c_pair", [128, 128])
        c_id = sb("c_id", [128, 128])
        alpha_sb = sb("alpha_sb", [128, 1])
        win_sb = sb("win_sb", [128, C2])
        win_hi = sb("win_hi", [128, C2], F16)
        win_lo = sb("win_lo", [128, C2], F16)
        wdw_sb = sb("wdw_sb", [HC, 2, 9])
        wdw_16 = sb("wdw_16", [HC, 2, 9], F16)
        wdw_hi = sb("wdw_hi", [HC, 2, 9])
        wdw_lo = sb("wdw_lo", [HC, 2, 9])
        filt_sb = sb("filt_sb", [NF, C2])
        wout_sb = sb("wout_sb", [HC, C])
        craw = sb("craw", [128, 9, C])
        cge = sb("cge", [128, 9, C])
        csign = sb("csign", [128, 4, 3, 128], F16)
        mult = sb("mult", [BPX, C2])
        N_PE = max(len(k) for k in PE_TAPS)
        diag_hi = sb("diag_hi", [HC, 2, N_PE, HC], F16)
        diag_lo = sb("diag_lo", [HC, 2, N_PE, HC], F16)

        X = sb("X", [128, H, W])
        S = sb("S", [128, H + 2, PITCH], F16)
        n32 = sb("n32", [128, 2, ROWS, W])
        junk = sb("junk", [128, NPX])
        sums = sb("sums", [128, 2, STRIPS])
        statx = sb("statx", [128, 2])
        ngmx = sb("ngmx", [128, 1])
        varx = sb("varx", [128, 1])
        vex = sb("vex", [128, 1])
        rstdx = sb("rstdx", [128, 1])
        nbx = sb("nbx", [128, 1])
        bn = sb("bn", [128, 2 * STRIPS, 6])
        mv = sb("mv", [128, 2])
        dev = sb("dev", [128, 1])
        m_half = sb("m_half", [128, 1])
        spread = sb("spread", [128, 1])
        gm1 = sb("gm1", [128, 1])
        ve1 = sb("ve1", [128, 1])
        rstd1 = sb("rstd1", [128, 1])
        nb1 = sb("nb1", [128, 1])

        xn = sb("xn", [128, NBLK, ROWS, BW])
        xT = sb("xT", [BPX, NBLK, 2, C])
        xf32 = sb("xf32", [128, NBLK, BPX])
        xf = sb("xf", [128, NBLK, BPX], F16)
        hf = sb("hf", [BPX, NBLK, C2])
        h = sb("h", [HC, 2, RING + 2, PITCH])
        h16 = sb("h16", [HC, 2, 2, RING, PITCH], F16)
        gel = sb("gel", [HC, NPX])
        g = sb("g", [HC, NPX])
        o = sb("o", [C, 2, NPX])

        PS = ctx.enter_context(nc.psum_tensor("PS", [128, 8, 512], F32))
        bank = [PS[:, i, :] for i in range(8)]

        def banks(a, n):
            return PS[:, a:a + 2, :].rearrange("p a b -> p (a b)")[:, 0:n]

        dma_const = sem("dma_const")
        dma_conv = sem("dma_conv")
        dma_x = [sem("dma_x_upper"), sem("dma_x_lower")]
        dma_out = [sem("dma_out0"), sem("dma_out1")]
        pool_zero = sem("pool_zero")
        pool_lo = sem("pool_lo")
        pool_rstdx = sem("pool_rstdx")
        pool_rstd1 = sem("pool_rstd1")
        pool_xf = sem("pool_xf")
        pool_h = sem("pool_h")
        dve_prep = sem("dve_prep")
        dve_csign = sem("dve_csign")
        dve_sq = sem("dve_sq")
        pe_mult = sem("pe_mult")
        pe_statx = sem("pe_statx")
        pe_stat1 = sem("pe_stat1")
        pe_conv = sem("pe_conv")
        pe_xT = sem("pe_xT")
        pe_xf = sem("pe_xf")
        pe_hf = sem("pe_hf")
        pe_h = sem("pe_h")
        pe_dwA = sem("pe_dwA")
        pe_dwB = sem("pe_dwB")
        pe_out = sem("pe_out")
        act_sum = sem("act_sum")
        act_statx = sem("act_statx")
        act_n32 = sem("act_n32")
        act_hi = sem("act_hi")
        act_xn = sem("act_xn")
        act_xT = sem("act_xT")
        act_xf = sem("act_xf")
        act_h = sem("act_h")
        act_h16 = sem("act_h16")
        act_gel = sem("act_gel")
        dve_statx = sem("dve_statx")
        dve_conv = sem("dve_conv")
        dve_bn = sem("dve_bn")
        dve_stat1 = sem("dve_stat1")
        dve_tap = sem("dve_tap")
        dve_hf = sem("dve_hf")
        dve_g = sem("dve_g")
        dve_o = sem("dve_o")
        N_CONST = 11

        BACK, DW, OUT = 1, 3, 4

        def spread_over(counts):
            steps, j = {}, 0
            for t, n in counts:
                steps[t] = list(range(j, j + n))
                j += n
            assert j == STRIPS
            return steps

        SUM_STEPS = spread_over([(2, 5), (3, 5), (4, 4)])
        SQ_STEPS = spread_over([(5, 7), (6, 7)])
        NORM_STEPS = spread_over([(8, 5), (9, 3), (10, 3), (11, 3)])
        CONV_STEPS = spread_over([(9, 3), (10, 3), (11, 3), (12, 3), (13, 2)])
        MEAN_STEP, VAR_STEP = 5, 7
        UPPER = 10
        CONV_BANK = [0, 1, 7]
        HF_AFTER, OUT_AFTER = 3, 3

        def item(b, t, lag, prev, front):
            if t >= lag:
                return (b, t - lag, 0) if front else None
            return (b - 1, t - lag + STRIPS, 1) if prev else None

        def tap_pieces(s, dy):
            rows = [i for i in range(ROWS) if 0 <= s * ROWS + i + dy < H]
            if len(rows) == ROWS:
                return [(0, ROWS)]
            return [(rows[0], HALF_ROWS), (HALF_ROWS, rows[-1] + 1)]

        TAP_OPS = [[sum(len(tap_pieces(s, dy)) for dy, _ in DVE_TAPS[half]) for half in range(2)]
                   for s in range(STRIPS)]
        TAPS_IMG = sum(map(sum, TAP_OPS))

        def tap_base(s, half):
            return sum(map(sum, TAP_OPS[:s])) + (TAP_OPS[s][0] if half else 0)

        def slot(parity, s):
            return (parity * STRIPS + s) % RING_STRIPS

        block = ctx.enter_context(nc.Block())

        @block.sync
        def _(sp):
            def load_x(b, parity, part):
                rows = slice(0, UPPER * ROWS) if part == 0 else slice(UPPER * ROWS, H)
                sp.dma_start(X[parity * C:(parity + 1) * C, rows, :].rearrange("p a b -> p (a b)"),
                             x[b, :, rows, :].rearrange("c a b -> c (a b)")).then_inc(dma_x[part], 16)

            for dst, src in ((c_fwd, forward), (c_inv, inverse), (c_pick, pick), (c_pair, pair), (c_id, identity),
                             (filt_sb, filt), (wout_sb, w_out)):
                sp.dma_start(dst[:], src).then_inc(dma_const, 16)
            load_x(0, 0, 0)
            load_x(0, 0, 1)
            sp.dma_start(wdw_sb[:], w_dw.rearrange("(a c) t -> c a t", a=2)).then_inc(dma_const, 16)
            sp.dma_start(win_sb[0:C], w_in).then_inc(dma_const, 16)
            sp.dma_start(win_sb[C:128], w_in).then_inc(dma_const, 16)
            sp.dma_start(alpha_sb[0:C], alpha).then_inc(dma_const, 16)
            sp.dma_start(craw[0:C], conv_w).then_inc(dma_conv, 16)
            sp.dma_start(craw[C:128], conv_w).then_inc(dma_conv, 16)
            sp.dma_start(alpha_sb[C:128], alpha).then_inc(dma_conv, 16)

            def image(b, parity, prev, front, more):
                for t in range(STRIPS if front else OUT):
                    if strip := item(b, t, OUT, prev, front):
                        bb, w, _ = strip
                        sp.wait_ge(dve_o, 2 * (bb * STRIPS + w) + 2)
                        sp.dma_start(out[bb, :, w * ROWS:(w + 1) * ROWS, :].rearrange("c a b -> c (a b)"),
                                     o[:, w % 2, :]).then_inc(dma_out[w % 2], 16)
                    if more and t == 0:
                        sp.wait_ge(act_sum, b * 2 * STRIPS + STRIPS)
                        load_x(b + 1, 1 - parity, 0)
                    if more and t == OUT - 1:
                        load_x(b + 1, 1 - parity, 1)

            image(0, 0, False, True, True)
            with sp.Fori(0, (B - 2) // 2) as pair_of:
                image(sp.snap(pair_of * 2 + 1), 1, True, True, True)
                image(sp.snap(pair_of * 2 + 2), 0, True, True, True)
            image(B - 1, 1, True, True, False)
            image(B, 0, True, False, False)
            sp.wait_ge(dma_out[0], B * 16 * (STRIPS // 2))
            sp.wait_ge(dma_out[1], B * 16 * (STRIPS // 2))

        @block.gpsimd
        def _(pool):
            nc.gpsimd.memset(S[:], 0.0).then_inc(pool_zero, 1)
            nc.gpsimd.memset(csign[:], 0.0).then_inc(pool_zero, 1)
            nc.gpsimd.memset(statx[:], 0.0).then_inc(pool_zero, 1)
            nc.gpsimd.memset(mv[:], 0.0).then_inc(pool_zero, 1)
            nc.gpsimd.memset(spread[:], 0.0).then_inc(pool_zero, 1)
            nc.gpsimd.memset(xn[:], 0.0).then_inc(pool_zero, 1)
            nc.gpsimd.memset(m_half[:], -0.5).then_inc(pool_zero, 1)
            nc.gpsimd.memset(h[:], 0.0).then_inc(pool_zero, 1)
            nc.gpsimd.memset(h16[:], 0.0).then_inc(pool_zero, 1)
            pool.wait_ge(pool_zero, 9)

            def rstd_x(b):
                pool.wait_ge(dve_statx, b * 4 + 3)
                nc.gpsimd.tensor_tensor(rstdx[:], vex[:], m_half[:], ALU.pow).then_inc(pool_rstdx, 1)

            def rstd_1(b):
                pool.wait_ge(dve_stat1, b * 6 + 5)
                nc.gpsimd.tensor_tensor(rstd1[:], ve1[:], m_half[:], ALU.pow).then_inc(pool_rstd1, 1)

            def low_part(b, parity, j):
                side = slice(parity * C, (parity + 1) * C)
                pool.wait_ge(act_hi, b * STRIPS + j + 1)
                rows = S[side, 1 + j * ROWS:1 + (j + 1) * ROWS, 1:1 + W]
                nc.gpsimd.tensor_tensor(rows, n32[side, j % 2], rows, ALU.subtract).then_inc(pool_lo, 1)

            def image(b, parity, prev, front, more):
                for t in range(STRIPS if front else BACK):
                    strip = item(b, t, BACK, prev, front)
                    if front and t == 0:
                        if prev:
                            pool.wait_ge(pool_h, 2 * (b * STRIPS - 1))
                        pool.wait_ge(pool_lo, b * STRIPS + STRIPS)
                        rstd_1(b)
                        pool.wait_ge(pool_rstd1, b + 1)
                    if front:
                        if t > BACK or (prev and t > 0):
                            pool.wait_ge(pool_h, 2 * (b * STRIPS + t - 1))
                        if more and t - 1 in NORM_STEPS:
                            pool.wait_ge(pool_lo, (b + 1) * STRIPS + NORM_STEPS[t - 1][-1] + 1)
                        if more and t - 1 == VAR_STEP:
                            pool.wait_ge(pool_rstdx, b + 2)
                        pool.wait_ge(act_xf, b * STRIPS + t + 1)
                        nc.gpsimd.tensor_tensor(xf[C:128], xf32[C:128], xf[C:128], ALU.subtract).then_inc(pool_xf, 1)
                        pool.wait_ge(pool_xf, b * STRIPS + t + 1)
                    if strip:
                        bb, i, back = strip
                        row = slot((parity + back) % 2, i) * ROWS
                        for half in range(2):
                            pool.wait_ge(act_h16, 2 * (bb * STRIPS + i) + half + 1)
                            nc.gpsimd.tensor_tensor(h16[:, 1, half, row:row + ROWS, 1:1 + W],
                                                    h[:, half, 1 + row:1 + row + ROWS, 1:1 + W],
                                                    h16[:, 0, half, row:row + ROWS, 1:1 + W],
                                                    ALU.subtract).then_inc(pool_h, 1)
                    if more and t == VAR_STEP:
                        rstd_x(b + 1)
                    if more and t in NORM_STEPS:
                        pool.wait_ge(pool_h, 2 * (b * STRIPS + t))
                        for j in NORM_STEPS[t]:
                            low_part(b + 1, 1 - parity, j)

            rstd_x(0)
            pool.wait_ge(pool_rstdx, 1)
            for j in range(STRIPS):
                low_part(0, 0, j)
            image(0, 0, False, True, True)
            with pool.Fori(0, (B - 2) // 2) as pair_of:
                image(pool.snap(pair_of * 2 + 1), 1, True, True, True)
                image(pool.snap(pair_of * 2 + 2), 0, True, True, True)
            image(B - 1, 1, True, True, False)
            image(B, 0, True, False, False)

        @block.scalar
        def _(act):
            def sum_strip(b, parity, j):
                side = slice(parity * C, (parity + 1) * C)
                if j == 0 or j == UPPER:
                    act.wait_ge(dma_x[j // UPPER], b * 16 + 16)
                nc.scalar.activation(junk[side], X[side, j * ROWS:(j + 1) * ROWS, :].rearrange("p a b -> p (a b)"),
                                     ACT.Copy, accum_out=sums[side, 0, j:j + 1]).then_inc(act_sum, 1)
                act.wait_ge(act_sum, b * 2 * STRIPS + j + 1)

            def square_strip(b, parity, j):
                side = slice(parity * C, (parity + 1) * C)
                if j == 0:
                    act.wait_ge(act_statx, b * 2 + 1)
                nc.scalar.activation(junk[side], X[side, j * ROWS:(j + 1) * ROWS, :].rearrange("p a b -> p (a b)"),
                                     ACT.Square, bias=ngmx[side], accum_out=sums[side, 1, j:j + 1]).then_inc(act_sum, 1)
                act.wait_ge(act_sum, b * 2 * STRIPS + STRIPS + j + 1)

            def mean_to_sbuf(b):
                act.wait_ge(pe_statx, b * 2 + 1)
                nc.scalar.mul(ngmx[:], bank[6][:, 0:1], -1.0 / IMG).then_inc(act_statx, 1)

            def variance_to_sbuf(b):
                act.wait_ge(pe_statx, b * 2 + 2)
                nc.scalar.mul(varx[:], bank[6][:, 0:1], 1.0 / IMG).then_inc(act_statx, 1)

            def normalise_strip(b, parity, j):
                side, other = (slice(q * C, (q + 1) * C) for q in (parity, 1 - parity))
                if j == 0:
                    act.wait_ge(dve_statx, b * 4 + 4)
                if j >= 2:
                    act.wait_ge(pool_lo, b * STRIPS + j - 1)
                nc.scalar.activation(n32[side, j % 2], X[side, j * ROWS:(j + 1) * ROWS, :], ACT.Identity,
                                     bias=nbx[side], scale=rstdx[side]).then_inc(act_n32, 1)
                act.wait_ge(act_n32, b * STRIPS + j + 1)
                nc.scalar.activation(S[other, 1 + j * ROWS:1 + (j + 1) * ROWS, 1:1 + W], n32[side, j % 2], ACT.Copy)
                nc.scalar.activation(S[side, 1 + j * ROWS:1 + (j + 1) * ROWS, 1:1 + W], n32[side, j % 2],
                                     ACT.Copy).then_inc(act_hi, 1)

            def image(b, parity, prev, front, more):
                side = slice(parity * C, (parity + 1) * C)

                def normalise_x1(m):
                    if m == 0:
                        act.wait_ge(dve_stat1, b * 6 + 6)
                    if prev or m:
                        act.wait_ge(pe_xT, b * STRIPS + m)
                    nc.scalar.activation(xn[0:C].rearrange("p k r c -> p r k c"),
                                         X[side, m * ROWS:(m + 1) * ROWS, :].rearrange("p r (k c) -> p r k c", c=BW),
                                         ACT.Identity, bias=nb1[side], scale=rstd1[side]).then_inc(act_xn, 1)

                for t in range(STRIPS if front else OUT):
                    back_strip = item(b, t, BACK, prev, front)
                    if back_strip:
                        bb, i, back = back_strip
                        at = slot((parity + back) % 2, i)
                        row = at * ROWS
                        for half in range(2):
                            if half == 0:
                                if i >= 3:
                                    act.wait_ge(dve_tap, bb * TAPS_IMG + tap_base(i - 2, 0))
                                elif back or prev:
                                    act.wait_ge(dve_tap, (bb - 1) * TAPS_IMG + tap_base(i + STRIPS - 2, 0))
                            act.wait_ge(pe_h, 2 * (bb * STRIPS + i) + half + 1)
                            src = banks(4 + 2 * half, NBLK * BPX).rearrange("p (k r c) -> p k r c", k=NBLK, r=ROWS)
                            if at == 0:
                                nc.scalar.activation(h[:, half, RING + 1, 1:1 + W].rearrange("p (k c) -> p k c", c=BW),
                                                     src[:, :, 0, :], ACT.Copy)
                            if at == RING_STRIPS - 1:
                                nc.scalar.activation(h[:, half, 0, 1:1 + W].rearrange("p (k c) -> p k c", c=BW),
                                                     src[:, :, ROWS - 1, :], ACT.Copy)
                            nc.scalar.activation(
                                h[:, half, 1 + row:1 + row + ROWS, 1:1 + W].rearrange("p r (k c) -> p k r c", c=BW),
                                src, ACT.Copy).then_inc(act_h, 1)
                    if front:
                        n = t
                        if n == 0:
                            normalise_x1(0)
                        act.wait_ge(pe_xT, b * STRIPS + n + 1)
                        if n or prev:
                            act.wait_ge(pe_xf, b * STRIPS + n)
                        nc.scalar.activation(xT[:], bank[4][:, 0:NBLK * C].rearrange("p (k c) -> p k c", c=C).unsqueeze(2)
                                             .broadcast_to([BPX, NBLK, 2, C]), ACT.Copy).then_inc(act_xT, 1)
                        if more and t == MEAN_STEP:
                            mean_to_sbuf(b + 1)
                        if more and t == VAR_STEP:
                            variance_to_sbuf(b + 1)
                    if strip := item(b, t, DW, prev, front):
                        bb, s, _ = strip
                        act.wait_ge(dve_tap, bb * TAPS_IMG + tap_base(s, 1))
                        if s or prev:
                            act.wait_ge(dve_g, bb * STRIPS + s)
                        nc.scalar.activation(gel[:].rearrange("p (a b) -> p a b", a=2), PS[:, 0:2, 0:TILE],
                                             ACT.Gelu).then_inc(act_gel, 1)
                    if front:
                        act.wait_ge(pe_xf, b * STRIPS + n + 1)
                        if n or prev:
                            act.wait_ge(pe_hf, 2 * (b * STRIPS + n))
                        spectrum = banks(6, NBLK * BPX).rearrange("p (k f) -> p k f", k=NBLK)
                        nc.scalar.activation(xf32[C:128], spectrum[C:128], ACT.Copy)
                        nc.scalar.activation(xf[:], spectrum, ACT.Copy).then_inc(act_xf, 1)
                    if back_strip:
                        bb, i, back = back_strip
                        for half in range(2):
                            act.wait_ge(act_h, 2 * (bb * STRIPS + i) + half + 1)
                            nc.scalar.activation(h16[:, 0, half, row:row + ROWS, 1:1 + W],
                                                 h[:, half, 1 + row:1 + row + ROWS, 1:1 + W],
                                                 ACT.Copy).then_inc(act_h16, 1)
                    if front and n + 1 < STRIPS:
                        normalise_x1(n + 1)
                    if more:
                        for j in SUM_STEPS.get(t, ()):
                            sum_strip(b + 1, 1 - parity, j)
                        for j in SQ_STEPS.get(t, ()):
                            square_strip(b + 1, 1 - parity, j)
                        for j in NORM_STEPS.get(t, ()):
                            normalise_strip(b + 1, 1 - parity, j)

            for j in range(STRIPS):
                sum_strip(0, 0, j)
            mean_to_sbuf(0)
            for j in range(STRIPS):
                square_strip(0, 0, j)
            variance_to_sbuf(0)
            act.wait_ge(pool_zero, 9)
            for j in range(STRIPS):
                normalise_strip(0, 0, j)
            image(0, 0, False, True, True)
            with act.Fori(0, (B - 2) // 2) as pair_of:
                image(act.snap(pair_of * 2 + 1), 1, True, True, True)
                image(act.snap(pair_of * 2 + 2), 0, True, True, True)
            image(B - 1, 1, True, True, False)
            image(B, 0, True, False, False)

        @block.vector
        def _(dve):
            dve.wait_ge(dma_conv, 48)
            nc.vector.tensor_scalar(cge[:], craw[:], 0.0, 2.0, ALU.is_ge, ALU.mult).then_inc(dve_sq, 1)
            dve.wait_ge(dve_sq, 1)
            dve.wait_ge(pool_zero, 9)
            for d in range(4):
                for odd in range(2):
                    ky = d - odd
                    if 0 <= ky < 3:
                        nc.vector.tensor_scalar(csign[:, d, :, odd * C:(odd + 1) * C], cge[:, 3 * ky:3 * ky + 3, :],
                                                1.0, None, ALU.subtract).then_inc(dve_csign, 1)
            dve.wait_ge(dma_const, 16 * N_CONST)
            nc.vector.tensor_copy(win_hi[:], win_sb[:]).then_inc(dve_sq, 1)
            nc.vector.tensor_copy(wdw_16[:], wdw_sb[:]).then_inc(dve_sq, 1)
            dve.wait_ge(dve_sq, 3)
            nc.vector.tensor_tensor(win_lo[:], win_sb[:], win_hi[:], ALU.subtract).then_inc(dve_prep, 1)
            nc.vector.tensor_copy(wdw_hi[:], wdw_16[:]).then_inc(dve_sq, 1)
            nc.vector.tensor_tensor(wdw_lo[:], wdw_sb[:], wdw_16[:], ALU.subtract).then_inc(dve_sq, 1)
            dve.wait_ge(dve_sq, 5)
            for half in range(2):
                for k, (dy, dx) in enumerate(PE_TAPS[half]):
                    at = (dy + 1) * 3 + dx + 1
                    nc.vector.tensor_scalar(diag_hi[:, half, k, :], c_id[:], wdw_hi[:, half, at:at + 1], None, ALU.mult)
                    nc.vector.tensor_scalar(diag_lo[:, half, k, :], c_id[:], wdw_lo[:, half, at:at + 1], None,
                                            ALU.mult).then_inc(dve_prep, 1)
            dve.wait_ge(pe_mult, 1)
            nc.vector.tensor_copy(mult[:], bank[5][:, 0:C2]).then_inc(dve_prep, 1)

            def sum_statx(b, parity):
                side = slice(parity * C, (parity + 1) * C)
                dve.wait_ge(act_sum, b * 2 * STRIPS + STRIPS)
                nc.vector.reduce_sum(statx[side, 0:1], sums[side, 0, :], axis=AX.X).then_inc(dve_statx, 1)

            def square_statx(b, parity):
                side = slice(parity * C, (parity + 1) * C)
                dve.wait_ge(act_sum, b * 2 * STRIPS + 2 * STRIPS)
                nc.vector.reduce_sum(statx[side, 1:2], sums[side, 1, :], axis=AX.X).then_inc(dve_statx, 1)

            def scale_statx(b):
                dve.wait_ge(act_statx, b * 2 + 2)
                nc.vector.tensor_scalar(vex[:], varx[:], GN_EPS, None, ALU.add).then_inc(dve_statx, 1)
                dve.wait_ge(pool_rstdx, b + 1)
                nc.vector.tensor_tensor(nbx[:], ngmx[:], rstdx[:], ALU.mult).then_inc(dve_statx, 1)

            def taps(bb, parity, s, half, which):
                base = bb * TAPS_IMG + tap_base(s, half)
                k = 0
                for n, (dy, dx) in enumerate(DVE_TAPS[half]):
                    at = (dy + 1) * 3 + dx + 1
                    for i0, i1 in tap_pieces(s, dy):
                        k += 1
                        if n not in which:
                            continue
                        if k > 1:
                            dve.wait_ge(dve_tap, base + k - 1)
                        elif half == 0:
                            dve.wait_ge(pe_dwA, bb * STRIPS + s + 1)
                        else:
                            dve.wait_ge(pe_dwB, bb * STRIPS + s + 1)
                        if dy == 1 and s + 1 < STRIPS and DVE_TAPS[half][n - 1][0] != 1:
                            dve.wait_ge(act_h, 2 * (bb * STRIPS + s + 1) + half + 1)
                        row = 1 + slot(parity, s) * ROWS + i0 + dy
                        src = h[:, half, row:row + i1 - i0, 1 + dx:1 + dx + W]
                        if i1 - i0 == ROWS:
                            acc = PS[:, 2 * half:2 * half + 2, 0:TILE].rearrange("p a (r c) -> p a r c", c=W)
                            src = src.rearrange("p (a r) c -> p a r c", a=2)
                        else:
                            q = i0 // HALF_ROWS
                            acc = bank[2 * half + q][:, (i0 - q * HALF_ROWS) * W:(i1 - q * HALF_ROWS) * W]
                            acc = acc.rearrange("p (r c) -> p r c", c=W)
                        nc.vector.scalar_tensor_tensor(out=acc, in0=src, scalar=wdw_sb[:, half, at:at + 1], in1=acc,
                                                       op0=ALU.mult, op1=ALU.add).then_inc(dve_tap, 1)

            def convolved(b, parity, strips):
                side = slice(parity * C, (parity + 1) * C)
                for j in strips:
                    dve.wait_ge(pe_conv, b * STRIPS + j + 1)
                    for odd in range(2):
                        rows = slice(j * ROWS + odd, (j + 1) * ROWS, 2)
                        nc.vector.scalar_tensor_tensor(
                            out=X[side, rows, :],
                            in0=bank[CONV_BANK[j % 3]][odd * C:(odd + 1) * C, 0:TILE].rearrange("p (r c) -> p r c", c=W),
                            scalar=alpha_sb[odd * C:(odd + 1) * C], in1=X[side, rows, :],
                            op0=ALU.mult, op1=ALU.add).then_inc(dve_conv, 1)
                for j in strips:
                    dve.wait_ge(dve_conv, 2 * (b * STRIPS + j) + 2)
                    for k in range(2):
                        row0 = j * ROWS + k * HALF_ROWS
                        nc.vector.bn_stats(bn[side, 2 * j + k, :],
                                           X[side, row0:row0 + HALF_ROWS, :].rearrange("p a b -> p (a b)")).then_inc(dve_bn, 1)
                if strips[-1] == STRIPS - 1:
                    other = slice((1 - parity) * C, (2 - parity) * C)
                    dve.wait_ge(dve_bn, 2 * (b * STRIPS + STRIPS))
                    nc.vector.memset(mv[other], 0.0)
                    nc.vector.bn_aggr(mv[side], bn[side].rearrange("p a b -> p (a b)")).then_inc(dve_stat1, 1)

            def group_variance(b):
                dve.wait_ge(pe_stat1, b * 2 + 1)
                nc.vector.tensor_tensor(dev[:], mv[:, 0:1], bank[2][:, 0:1], ALU.subtract).then_inc(dve_stat1, 1)
                nc.vector.tensor_copy(gm1[:], bank[2][:, 0:1]).then_inc(dve_stat1, 1)
                dve.wait_ge(dve_stat1, b * 6 + 3)
                nc.vector.scalar_tensor_tensor(out=spread[:], in0=dev[:], scalar=dev[:], in1=mv[:, 1:2],
                                               op0=ALU.mult, op1=ALU.add).then_inc(dve_stat1, 1)

            def image(b, parity, prev, front, more):
                side = slice(parity * C, (parity + 1) * C)
                for t in range(STRIPS if front else OUT):
                    if t == 0 and front:
                        group_variance(b)
                    dw = item(b, t, DW, prev, front)
                    back_strip = item(b, t, BACK, prev, front)
                    if dw:
                        bb, s, back = dw
                        par = (parity + back) % 2
                        taps(bb, par, s, 0, range(0, 1))
                    if t == 0 and front:
                        dve.wait_ge(pe_stat1, b * 2 + 2)
                        nc.vector.tensor_scalar(ve1[:], bank[3][:, 0:1], GN_EPS, None, ALU.add).then_inc(dve_stat1, 1)
                    if dw:
                        taps(bb, par, s, 0, range(1, HF_AFTER))
                    if back_strip:
                        fb, i, _ = back_strip
                        if i or back_strip[2] or prev:
                            dve.wait_ge(pe_h, 2 * (fb * STRIPS + i))
                        for part, (at, k0, k1) in enumerate(((6, 0, 4), (4, 4, NBLK))):
                            dve.wait_ge(pe_hf, 2 * (fb * STRIPS + i) + part + 1)
                            nc.vector.tensor_tensor(
                                hf[:, k0:k1, :], banks(at, (k1 - k0) * C2).rearrange("p (k c) -> p k c", c=C2),
                                mult[:].unsqueeze(1).broadcast_to([BPX, k1 - k0, C2]), ALU.mult).then_inc(dve_hf, 1)
                    if t == 0 and front:
                        dve.wait_ge(pool_rstd1, b + 1)
                        nc.vector.scalar_tensor_tensor(out=nb1[:], in0=gm1[:], scalar=-1.0, in1=rstd1[:],
                                                       op0=ALU.mult, op1=ALU.mult).then_inc(dve_stat1, 1)
                    if dw:
                        taps(bb, par, s, 0, range(HF_AFTER, 9))
                        taps(bb, par, s, 1, range(0, OUT_AFTER))
                    if strip := item(b, t, OUT, prev, front):
                        wb, w, back = strip
                        wside = slice((parity + back) % 2 * C, ((parity + back) % 2 + 1) * C)
                        dve.wait_ge(pe_out, wb * STRIPS + w + 1)
                        if w >= 2 or prev:
                            dve.wait_ge(dma_out[w % 2], 16 * (wb * (STRIPS // 2) + w // 2))
                        for q in range(2):
                            nc.vector.tensor_tensor(
                                o[:, w % 2, q * TILE:(q + 1) * TILE], bank[5][q * C:(q + 1) * C, 0:TILE],
                                X[wside, w * ROWS + q * HALF_ROWS:w * ROWS + (q + 1) * HALF_ROWS, :].rearrange(
                                    "p r c -> p (r c)"), ALU.add).then_inc(dve_o, 1)
                    if dw:
                        taps(bb, par, s, 1, range(OUT_AFTER, 9))
                        dve.wait_ge(dve_tap, bb * TAPS_IMG + tap_base(s, 1) + TAP_OPS[s][1])
                        dve.wait_ge(act_gel, bb * STRIPS + s + 1)
                        if s or prev:
                            dve.wait_ge(pe_out, bb * STRIPS + s)
                        nc.vector.tensor_tensor(g[:].rearrange("p (a b) -> p a b", a=2),
                                                gel[:].rearrange("p (a b) -> p a b", a=2), PS[:, 2:4, 0:TILE],
                                                ALU.mult).then_inc(dve_g, 1)
                    if more and t in CONV_STEPS:
                        convolved(b + 1, 1 - parity, CONV_STEPS[t])
                    if more and t == max(SUM_STEPS):
                        sum_statx(b + 1, 1 - parity)
                    if more and t == max(SQ_STEPS):
                        square_statx(b + 1, 1 - parity)
                    if more and t == VAR_STEP:
                        scale_statx(b + 1)

            sum_statx(0, 0)
            square_statx(0, 0)
            scale_statx(0)
            convolved(0, 0, range(STRIPS))
            image(0, 0, False, True, True)
            with dve.Fori(0, (B - 2) // 2) as pair_of:
                image(dve.snap(pair_of * 2 + 1), 1, True, True, True)
                image(dve.snap(pair_of * 2 + 2), 0, True, True, True)
            image(B - 1, 1, True, True, False)
            image(B, 0, True, False, False)

        @block.tensor
        def _(pe):
            def mean_x(b):
                pe.wait_ge(dve_statx, b * 4 + 1)
                nc.tensor.matmul(bank[6][:, 0:1], c_pair[:], statx[:, 0:1], start=True, stop=True).then_inc(pe_statx, 1)

            def variance_x(b):
                pe.wait_ge(dve_statx, b * 4 + 2)
                nc.tensor.matmul(bank[6][:, 0:1], c_pair[:], statx[:, 1:2], start=True, stop=True).then_inc(pe_statx, 1)

            def convolution(b, strips):
                for j in strips:
                    pe.wait_ge(pool_lo, b * STRIPS + min(j + 2, STRIPS))
                    if j >= 3:
                        pe.wait_ge(dve_conv, 2 * (b * STRIPS + j - 2))
                    for d in range(4):
                        for kx in range(3):
                            row0 = j * ROWS + d
                            last = nc.tensor.matmul(bank[CONV_BANK[j % 3]][:, 0:TILE], csign[:, d, kx, :],
                                                    S[:, row0:row0 + ROWS - 1:2, kx:kx + W],
                                                    start=(d == 0 and kx == 0), stop=(d == 3 and kx == 2))
                    last.then_inc(pe_conv, 1)

            def depthwise(parity, s, half):
                for q in range(2):
                    todo = []
                    for k, (dy, dx) in enumerate(PE_TAPS[half]):
                        rows = [i for i in range(q * HALF_ROWS, (q + 1) * HALF_ROWS) if 0 <= s * ROWS + i + dy < H]
                        first = (slot(parity, s) * ROWS + rows[0] + dy) % RING
                        cut = min(len(rows), RING - first)
                        for i0, n, row in ((rows[0], cut, first), (rows[0] + cut, len(rows) - cut, 0)):
                            if n > 0:
                                at = (i0 - q * HALF_ROWS) * W
                                for data, weights in ((0, diag_hi), (1, diag_hi), (0, diag_lo)):
                                    todo.append((bank[2 * half + q][:, at:at + n * W], weights[:, half, k, :],
                                                 h16[:, data, half, row:row + n, 1 + dx:1 + dx + W]))
                    for m, (acc, weights, rows) in enumerate(todo):
                        last = nc.tensor.matmul(acc, weights, rows, start=(m == 0), stop=(m == len(todo) - 1),
                                                skip_group_check=True)
                return last

            pe.wait_ge(dma_const, 16 * N_CONST)
            nc.tensor.matmul(bank[5][:, 0:C2], c_pick[:], filt_sb[:], start=True, stop=True).then_inc(pe_mult, 1)
            pe.wait_ge(pool_zero, 9)
            mean_x(0)
            pe.wait_ge(act_statx, 1)
            variance_x(0)
            pe.wait_ge(dve_csign, 6)
            pe.wait_ge(act_statx, 2)
            convolution(0, range(STRIPS))
            pe.wait_ge(dve_prep, sum(map(len, PE_TAPS)) + 2)

            def image(b, parity, prev, front, more):
                for t in range(STRIPS if front else OUT):
                    back_strip = item(b, t, BACK, prev, front)
                    dw = item(b, t, DW, prev, front)
                    out_strip = item(b, t, OUT, prev, front)
                    conv_done = None
                    if t == 0 and front:
                        conv_done = 2 * (b * STRIPS + STRIPS)
                    elif more and t - 1 in CONV_STEPS:
                        conv_done = 2 * ((b + 1) * STRIPS + CONV_STEPS[t - 1][-1] + 1)
                    if dw:
                        bb, s, back = dw
                        pe.wait_ge(pool_h, 2 * (bb * STRIPS + s) + 2)
                        if conv_done is not None:
                            pe.wait_ge(dve_conv, conv_done)
                        if s or prev:
                            pe.wait_ge(act_gel, bb * STRIPS + s)
                        depthwise((parity + back) % 2, s, 0).then_inc(pe_dwA, 1)
                    if t == 0 and front:
                        pe.wait_ge(dve_stat1, b * 6 + 1)
                        if prev:
                            pe.wait_ge(dve_g, bb * STRIPS + s)
                        nc.tensor.matmul(bank[2][:, 0:1], c_pair[:], mv[:, 0:1], start=True, stop=True).then_inc(pe_stat1, 1)
                    if back_strip:
                        bb, i, _ = back_strip
                        pe.wait_ge(pool_xf, bb * STRIPS + i + 1)
                        if conv_done is not None:
                            pe.wait_ge(dve_conv, conv_done)
                        for at, k0, k1 in ((6, 0, 4), (4, 4, NBLK)):
                            if at == 4 and (t > OUT or prev):
                                pe.wait_ge(dve_o, 2 * (b * STRIPS + t - OUT))
                            for k in range(k0, k1):
                                for weights in (win_hi, win_lo):
                                    last = nc.tensor.matmul(banks(at, (k1 - k0) * C2)[:, (k - k0) * C2:(k - k0 + 1) * C2],
                                                            xf[:, k, :], weights[:], start=weights is win_hi,
                                                            stop=weights is win_lo)
                            last.then_inc(pe_hf, 1)
                    if t == 0 and front:
                        pe.wait_ge(dve_stat1, b * 6 + 4)
                        nc.tensor.matmul(bank[3][:, 0:1], c_pair[:], spread[:], start=True, stop=True).then_inc(pe_stat1, 1)
                        pe.wait_ge(dve_stat1, b * 6 + 5)
                    if dw:
                        bb, s, back = dw
                        if s or prev:
                            pe.wait_ge(dve_g, bb * STRIPS + s)
                        depthwise((parity + back) % 2, s, 1).then_inc(pe_dwB, 1)
                    if back_strip:
                        bb, i, _ = back_strip
                        pe.wait_ge(dve_hf, 2 * (bb * STRIPS + i) + 2)
                        for half in range(2):
                            for k in range(NBLK):
                                last = nc.tensor.matmul(banks(4 + 2 * half, NBLK * BPX)[:, k * BPX:(k + 1) * BPX],
                                                        hf[:, k, half * HC:(half + 1) * HC], c_inv[:],
                                                        start=True, stop=True)
                            last.then_inc(pe_h, 1)

                    def transposed():
                        if back_strip:
                            pe.wait_ge(act_h, 2 * (back_strip[0] * STRIPS + back_strip[1]) + 1)
                        pe.wait_ge(act_xn, b * STRIPS + t + 1)
                        nc.tensor.transpose(bank[4][:, (NBLK - 1) * C:(NBLK + 1) * C],
                                            xn[:, NBLK - 1].rearrange("p r c -> p (r c)"), c_id[:])
                        for k in range(NBLK - 1):
                            last = nc.tensor.transpose(bank[4][:, k * C:(k + 1) * C],
                                                       xn[0:C, k].rearrange("p r c -> p (r c)"), c_id[0:C, 0:C])
                        last.then_inc(pe_xT, 1)

                    if front and t > 0:
                        transposed()
                    if out_strip:
                        bb, w, _ = out_strip
                        pe.wait_ge(dve_g, bb * STRIPS + w + 1)
                        if back_strip:
                            pe.wait_ge(act_h, 2 * (back_strip[0] * STRIPS + back_strip[1]) + 1)
                        elif w:
                            pe.wait_ge(dve_o, 2 * (bb * STRIPS + w))
                        for q in range(2):
                            last = nc.tensor.matmul(bank[5][q * C:(q + 1) * C, 0:TILE], wout_sb[:],
                                                    g[:, q * TILE:(q + 1) * TILE], start=True, stop=True)
                        last.then_inc(pe_out, 1)
                    if front and t == 0:
                        transposed()
                    if front:
                        if back_strip:
                            pe.wait_ge(act_h, 2 * (back_strip[0] * STRIPS + back_strip[1]) + 2)
                        if more and t == MEAN_STEP:
                            mean_x(b + 1)
                            pe.wait_ge(act_statx, (b + 1) * 2 + 1)
                        if more and t == VAR_STEP:
                            variance_x(b + 1)
                            pe.wait_ge(act_statx, (b + 1) * 2 + 2)
                        pe.wait_ge(act_xT, b * STRIPS + t + 1)
                        for k in range(NBLK):
                            last = nc.tensor.matmul(banks(6, NBLK * BPX)[:, k * BPX:(k + 1) * BPX],
                                                    xT[:, k].rearrange("p a c -> p (a c)"), c_fwd[:], start=True, stop=True)
                        last.then_inc(pe_xf, 1)
                    if more and t in CONV_STEPS:
                        pe.wait_ge(act_gel, dw[0] * STRIPS + dw[1] + 1)
                        if len(CONV_STEPS[t]) > 2:
                            pe.wait_ge(act_xf, b * STRIPS + t + 1)
                        convolution(b + 1, CONV_STEPS[t])

            image(0, 0, False, True, True)
            with pe.Fori(0, (B - 2) // 2) as pair_of:
                image(pe.snap(pair_of * 2 + 1), 1, True, True, True)
                image(pe.snap(pair_of * 2 + 2), 0, True, True, True)
            image(B - 1, 1, True, True, False)
            image(B, 0, True, False, False)


def kernel(x, L0_conv_weight, L0_conv_alpha, L1_conv_w_in, L1_conv_w_dw, L1_conv_fft_filt, L1_conv_w_out):
    import concourse.bacc as bacc
    from concourse.bass_utils import run_bass_kernel_spmd

    nc = bacc.Bacc("TRN2", target_bir_lowering=False, num_devices=1)
    nc.disable_value_cache = True
    arrays = {
        "x": np.ascontiguousarray(x),
        "conv_w": np.ascontiguousarray(np.transpose(np.asarray(L0_conv_weight), (1, 2, 3, 0))).reshape(C, 9, C),
        "alpha": np.ascontiguousarray(L0_conv_alpha).reshape(C, 1),
        "w_in": np.ascontiguousarray(np.transpose(np.asarray(L1_conv_w_in))),
        "w_dw": np.ascontiguousarray(L1_conv_w_dw).reshape(C2, 9),
        "filt": np.ascontiguousarray(np.transpose(np.asarray(L1_conv_fft_filt).reshape(C2, P * (P // 2 + 1)))),
        "w_out": np.ascontiguousarray(np.transpose(np.asarray(L1_conv_w_out))),
    }
    for name, a in shape_constants().items():
        arrays[name] = np.ascontiguousarray(a, dtype=np.float32)
    aps = {name: nc.dram_tensor(f"in_{name}", a.shape, F32, kind="ExternalInput").ap() for name, a in arrays.items()}
    out = nc.dram_tensor("out_x", arrays["x"].shape, F32, kind="ExternalOutput").ap()
    build(nc, *aps.values(), out)
    ran = run_bass_kernel_spmd(nc, [{f"in_{name}": a for name, a in arrays.items()}], core_ids=[0])
    return ran.results[0]["out_x"]
```

```python
import numpy as np
import concourse.bass as bass
from concourse import mybir
from contextlib import ExitStack

F32 = mybir.dt.float32
F16 = mybir.dt.float16
ACT = mybir.ActivationFunctionType
ALU = mybir.AluOpType
AX = mybir.AxisListType

P = 8
C = 64
C2 = 256
HC = 128
ROWS = P
BW = 2 * P
BPX = P * BW
GN_EPS = 1e-5
RING_STRIPS = 4
ALL_TAPS = [(dy, dx) for dy in (-1, 0, 1) for dx in (-1, 0, 1)]
PE_TAPS = [[(0, 0), (0, -1), (0, 1), (-1, 0)], [(0, 0), (0, -1), (0, 1)]]
DVE_TAPS = [[tap for tap in ALL_TAPS if tap not in taps] for taps in PE_TAPS]


def patch_basis():
    r, s = np.meshgrid(np.arange(P), np.arange(P), indexing="ij")
    columns, picks = [], []
    for k2 in range(P // 2 + 1):
        edge = k2 in (0, P // 2)
        for k1 in range(P // 2 + 1 if edge else P):
            angle = 2 * np.pi * (k1 * r + k2 * s) / P
            mirror = (-k1) % P if edge else k1
            for wave in (np.cos(angle), np.sin(angle)):
                norm = np.sqrt((wave ** 2).sum())
                if norm > 1e-6:
                    columns.append((wave / norm).reshape(-1))
                    picks.append((k1 * (P // 2 + 1) + k2, mirror * (P // 2 + 1) + k2))
    basis = np.stack(columns, axis=1)
    assert basis.shape == (P * P, P * P) and np.allclose(basis.T @ basis, np.eye(P * P))
    return basis, picks


def shape_constants():
    basis, picks = patch_basis()
    px = [(r * BW + patch * P + s) for patch in range(2) for r in range(P) for s in range(P)]
    forward = np.zeros((BPX, BPX))
    pick = np.zeros((P * (P // 2 + 1), BPX))
    for patch in range(2):
        at = px[patch * P * P:(patch + 1) * P * P]
        forward[np.ix_(at, range(patch * P * P, (patch + 1) * P * P))] = basis
        for f, (a, b) in enumerate(picks):
            pick[a, patch * P * P + f] += 0.5
            pick[b, patch * P * P + f] += 0.5
    pair = np.kron(np.eye(HC // 2), np.full((2, 2), 0.5))
    apart = np.eye(HC) - pair
    return {"forward": forward, "inverse": forward.T, "pick": pick, "pair": pair, "apart": apart, "identity": np.eye(HC)}


def build(nc, x, conv_w, alpha, w_in, w_dw, filt, w_out, forward, inverse, pick, pair, apart, identity, out):
    B, _, H, W = x.shape
    STRIPS = H // ROWS
    NBLK = W // BW
    NPX = ROWS * W
    TILE = NPX // 2
    HALF_ROWS = ROWS // 2
    PITCH = W + 2
    RING = RING_STRIPS * ROWS
    NF = P * (P // 2 + 1)
    IMG = H * W
    N32_BUFS = 3
    assert B % 2 == 0 and (2 * STRIPS) % RING_STRIPS == 0

    ctx = ExitStack()
    with ctx:
        def sb(name, shape, dt=F32):
            return ctx.enter_context(nc.sbuf_tensor(name, shape, dt))

        def sem(name):
            return ctx.enter_context(nc.semaphore(name))

        c_fwd = sb("c_fwd", [BPX, BPX])
        c_inv = sb("c_inv", [BPX, BPX])
        c_pick = sb("c_pick", [NF, BPX])
        c_pair = sb("c_pair", [128, 128])
        c_apart = sb("c_apart", [128, 128])
        c_id = sb("c_id", [128, 128])
        alpha_sb = sb("alpha_sb", [128, 1])
        win_sb = sb("win_sb", [128, C2])
        win_hi = sb("win_hi", [128, C2], F16)
        win_lo = sb("win_lo", [128, C2], F16)
        wdw_sb = sb("wdw_sb", [HC, 2, 9])
        wdw_16 = sb("wdw_16", [HC, 2, 9], F16)
        wdw_hi = sb("wdw_hi", [HC, 2, 9])
        wdw_lo = sb("wdw_lo", [HC, 2, 9])
        filt_sb = sb("filt_sb", [NF, C2])
        wout_sb = sb("wout_sb", [HC, C])
        craw = sb("craw", [128, 9, C])
        cge = sb("cge", [128, 9, C])
        csign = sb("csign", [128, 4, 3, 128], F16)
        mult = sb("mult", [BPX, C2])
        N_PE = max(len(k) for k in PE_TAPS)
        diag_hi = sb("diag_hi", [HC, 2, N_PE, HC], F16)
        diag_lo = sb("diag_lo", [HC, 2, N_PE, HC], F16)

        X = sb("X", [128, H, W])
        S = sb("S", [128, H + 2, PITCH], F16)
        n32 = sb("n32", [128, N32_BUFS, ROWS, W])
        bnx = sb("bnx", [128, 2, 6])
        firstx = sb("firstx", [128, 2])
        sums = sb("sums", [128, 2, STRIPS])
        totals = sb("totals", [128, 2])
        offset = sb("offset", [128, 2])
        junk = sb("junk", [128, NPX])
        mvx = sb("mvx", [128, 2])
        groupx = sb("groupx", [128, 3])
        varx = sb("varx", [128, 1])
        vex = sb("vex", [128, 1])
        rstdx = sb("rstdx", [128, 1])
        nbx = sb("nbx", [128, 1])
        bn = sb("bn", [128, 2 * STRIPS, 6])
        mv = sb("mv", [128, 2])
        m_half = sb("m_half", [128, 1])
        group1 = sb("group1", [128, 3])
        var1 = sb("var1", [128, 1])
        ve1 = sb("ve1", [128, 1])
        rstd1 = sb("rstd1", [128, 1])
        nb1 = sb("nb1", [128, 1])

        xn = sb("xn", [128, NBLK, ROWS, BW])
        xT = sb("xT", [BPX, NBLK, 2, C])
        xf32 = sb("xf32", [128, NBLK, BPX])
        xf = sb("xf", [128, NBLK, BPX], F16)
        hf = sb("hf", [BPX, NBLK, C2])
        h = sb("h", [HC, 2, RING + 2, PITCH])
        h16 = sb("h16", [HC, 2, 2, RING, PITCH], F16)
        gel = sb("gel", [HC, NPX])
        g = sb("g", [HC, NPX])
        o = sb("o", [128, 2, NPX])

        PS = ctx.enter_context(nc.psum_tensor("PS", [128, 8, 512], F32))
        bank = [PS[:, i, :] for i in range(8)]

        def banks(a, n):
            return PS[:, a:a + 2, :].rearrange("p a b -> p (a b)")[:, 0:n]

        dma_const = sem("dma_const")
        dma_conv = sem("dma_conv")
        dma_x = [sem(f"dma_x{part}") for part in range(4)]
        dma_out = [sem("dma_out0"), sem("dma_out1")]
        pool_zero = sem("pool_zero")
        pool_lo = sem("pool_lo")
        pool_rstdx = sem("pool_rstdx")
        pool_rstd1 = sem("pool_rstd1")
        pool_xf = sem("pool_xf")
        pool_h = sem("pool_h")
        pool_g = sem("pool_g")
        pool_o = sem("pool_o")
        dve_prep = sem("dve_prep")
        dve_csign = sem("dve_csign")
        dve_sq = sem("dve_sq")
        pe_mult = sem("pe_mult")
        pe_statx = sem("pe_statx")
        pe_stat1 = sem("pe_stat1")
        pe_conv = sem("pe_conv")
        pe_xT = sem("pe_xT")
        pe_xf = sem("pe_xf")
        pe_hf = sem("pe_hf")
        pe_h = sem("pe_h")
        pe_dwA = sem("pe_dwA")
        pe_dwB = sem("pe_dwB")
        pe_out = sem("pe_out")
        act_sum = sem("act_sum")
        act_statx = sem("act_statx")
        act_hi = sem("act_hi")
        act_xn = sem("act_xn")
        act_xT = sem("act_xT")
        act_xf = sem("act_xf")
        act_h = sem("act_h")
        act_h16 = sem("act_h16")
        act_gel = sem("act_gel")
        act_g = sem("act_g")
        act_o = sem("act_o")
        dve_bnx = sem("dve_bnx")
        dve_sums = sem("dve_sums")
        dve_statx = sem("dve_statx")
        dve_conv = sem("dve_conv")
        dve_bn = sem("dve_bn")
        dve_stat1 = sem("dve_stat1")
        dve_tap = sem("dve_tap")
        dve_hf = sem("dve_hf")
        N_CONST = 12

        BACK, DW, OUT = 1, 3, 4

        def spread_over(counts):
            steps, j = {}, 0
            for t, n in counts:
                steps[t] = list(range(j, j + n))
                j += n
            assert j == STRIPS
            return steps

        STAT_STEPS = {0: [(0, j) for j in range(3)], 1: [(0, j) for j in range(3, 8)],
                      2: [(1, j) for j in range(5)], 3: [(0, 8), (0, 9), (1, 5), (1, 6), (1, 7)],
                      4: [(0, 10), (0, 11), (1, 8), (1, 9), (1, 10)],
                      5: [(0, 12), (0, 13)] + [(1, j) for j in range(11, STRIPS)]}
        NORM_STEPS = spread_over([(7, 1), (8, 2), (9, 3), (10, 3), (11, 3), (12, 2)])
        CONV_STEPS = spread_over([(9, 2), (10, 3), (11, 3), (12, 3), (13, 3)])
        GROUP_STEP = 6
        LOADS = [(0, 0, 3), (0, 3, STRIPS - OUT), (2, STRIPS - OUT, 13), (3, 13, STRIPS)]

        def conv_bank(strips, pos):
            return (0, 7)[pos] if len(strips) == 2 else (0, 1, 7)[pos % 3]

        HF_AFTER = 2

        def item(b, t, lag, prev, front):
            if t >= lag:
                return (b, t - lag, 0) if front else None
            return (b - 1, t - lag + STRIPS, 1) if prev else None

        def tap_pieces(s, dy):
            rows = [i for i in range(ROWS) if 0 <= s * ROWS + i + dy < H]
            if len(rows) == ROWS:
                return [(0, ROWS)]
            return [(rows[0], HALF_ROWS), (HALF_ROWS, rows[-1] + 1)]

        TAP_OPS = [[sum(len(tap_pieces(s, dy)) for dy, _ in DVE_TAPS[half]) for half in range(2)]
                   for s in range(STRIPS)]
        TAPS_IMG = sum(map(sum, TAP_OPS))

        def tap_base(s, half):
            return sum(map(sum, TAP_OPS[:s])) + (TAP_OPS[s][0] if half else 0)

        def slot(parity, s):
            return (parity * STRIPS + s) % RING_STRIPS

        block = ctx.enter_context(nc.Block())

        @block.sync
        def _(sp):
            def load_x(b, parity, part):
                rows = slice(LOADS[part][1] * ROWS, LOADS[part][2] * ROWS)
                sp.dma_start(X[parity * C:(parity + 1) * C, rows, :].rearrange("p a b -> p (a b)"),
                             x[b, :, rows, :].rearrange("c a b -> c (a b)")).then_inc(dma_x[part], 16)

            for dst, src in ((c_fwd, forward), (c_inv, inverse), (c_pick, pick), (c_pair, pair), (c_apart, apart),
                             (c_id, identity), (filt_sb, filt), (wout_sb, w_out)):
                sp.dma_start(dst[:], src).then_inc(dma_const, 16)
            for part in range(len(LOADS)):
                load_x(0, 0, part)
            sp.dma_start(wdw_sb[:], w_dw.rearrange("(a c) t -> c a t", a=2)).then_inc(dma_const, 16)
            sp.dma_start(win_sb[0:C], w_in).then_inc(dma_const, 16)
            sp.dma_start(win_sb[C:128], w_in).then_inc(dma_const, 16)
            sp.dma_start(alpha_sb[0:C], alpha).then_inc(dma_const, 16)
            sp.dma_start(craw[0:C], conv_w).then_inc(dma_conv, 16)
            sp.dma_start(craw[C:128], conv_w).then_inc(dma_conv, 16)
            sp.dma_start(alpha_sb[C:128], alpha).then_inc(dma_conv, 16)

            def image(b, parity, prev, front, more):
                for t in range(STRIPS if front else OUT):
                    if more and t == 0:
                        sp.wait_ge(act_sum, b * 2 * STRIPS + 2 * STRIPS)
                        load_x(b + 1, 1 - parity, 0)
                        load_x(b + 1, 1 - parity, 1)
                    if strip := item(b, t, OUT, prev, front):
                        bb, w, back = strip
                        side = slice((parity + back) % 2 * C, ((parity + back) % 2 + 1) * C)
                        sp.wait_ge(pool_o, bb * STRIPS + w + 1)
                        sp.dma_start(out[bb, :, w * ROWS:(w + 1) * ROWS, :].rearrange("c a b -> c (a b)"),
                                     o[side, w % 2, :]).then_inc(dma_out[w % 2], 16)
                    for part in range(2, len(LOADS)):
                        if more and t == LOADS[part][0]:
                            load_x(b + 1, 1 - parity, part)

            image(0, 0, False, True, True)
            with sp.Fori(0, (B - 2) // 2) as pair_of:
                image(sp.snap(pair_of * 2 + 1), 1, True, True, True)
                image(sp.snap(pair_of * 2 + 2), 0, True, True, True)
            image(B - 1, 1, True, True, False)
            image(B, 0, True, False, False)
            sp.wait_ge(dma_out[0], B * 16 * (STRIPS // 2))
            sp.wait_ge(dma_out[1], B * 16 * (STRIPS // 2))

        @block.gpsimd
        def _(pool):
            nc.gpsimd.memset(S[:], 0.0).then_inc(pool_zero, 1)
            nc.gpsimd.memset(csign[:], 0.0).then_inc(pool_zero, 1)
            nc.gpsimd.memset(mvx[:], 0.0).then_inc(pool_zero, 1)
            nc.gpsimd.memset(mv[:], 0.0).then_inc(pool_zero, 1)
            nc.gpsimd.memset(xn[:], 0.0).then_inc(pool_zero, 1)
            nc.gpsimd.memset(m_half[:], -0.5).then_inc(pool_zero, 1)
            nc.gpsimd.memset(h[:], 0.0).then_inc(pool_zero, 1)
            nc.gpsimd.memset(h16[:], 0.0).then_inc(pool_zero, 1)
            pool.wait_ge(pool_zero, 8)

            def rstd_x(b):
                pool.wait_ge(dve_statx, b * 4 + 3)
                nc.gpsimd.tensor_tensor(rstdx[:], vex[:], m_half[:], ALU.pow).then_inc(pool_rstdx, 1)

            def rstd_1(b):
                pool.wait_ge(dve_stat1, b * 5 + 4)
                nc.gpsimd.tensor_tensor(rstd1[:], ve1[:], m_half[:], ALU.pow).then_inc(pool_rstd1, 1)

            def low_part(b, parity, j):
                side = slice(parity * C, (parity + 1) * C)
                pool.wait_ge(act_hi, b * STRIPS + j + 1)
                rows = S[side, 1 + j * ROWS:1 + (j + 1) * ROWS, 1:1 + W]
                nc.gpsimd.tensor_tensor(rows, n32[side, j % N32_BUFS], rows, ALU.subtract).then_inc(pool_lo, 1)

            def image(b, parity, prev, front, more):
                for t in range(STRIPS if front else OUT):
                    strip = item(b, t, BACK, prev, front)
                    out_strip = item(b, t, OUT, prev, front)
                    dw = item(b, t, DW, prev, front)
                    if front and t == 0:
                        if prev:
                            pool.wait_ge(pool_g, b * STRIPS - DW)
                        pool.wait_ge(pool_lo, b * STRIPS + STRIPS)
                        rstd_1(b)
                        pool.wait_ge(pool_rstd1, b + 1)
                    if front:
                        if t == 0:
                            pass
                        elif t > DW or prev:
                            pool.wait_ge(pool_g, b * STRIPS + t - DW)
                        elif t > BACK:
                            pool.wait_ge(pool_h, 2 * (b * STRIPS + t - 1))
                        if more and t - 1 in NORM_STEPS:
                            pool.wait_ge(pool_lo, (b + 1) * STRIPS + NORM_STEPS[t - 1][-1] + 1)
                        if more and t - 1 == GROUP_STEP:
                            pool.wait_ge(pool_rstdx, b + 2)
                        pool.wait_ge(act_xf, b * STRIPS + t + 1)
                        nc.gpsimd.tensor_tensor(xf[C:128], xf32[C:128], xf[C:128], ALU.subtract).then_inc(pool_xf, 1)
                        pool.wait_ge(pool_xf, b * STRIPS + t + 1)
                    if strip:
                        bb, i, h_back = strip
                        row = slot((parity + h_back) % 2, i) * ROWS
                        for half in range(2):
                            pool.wait_ge(act_h16, 2 * (bb * STRIPS + i) + half + 1)
                            nc.gpsimd.tensor_tensor(h16[:, 1, half, row:row + ROWS, 1:1 + W],
                                                    h[:, half, 1 + row:1 + row + ROWS, 1:1 + W],
                                                    h16[:, 0, half, row:row + ROWS, 1:1 + W],
                                                    ALU.subtract).then_inc(pool_h, 1)
                    if out_strip:
                        wb, w, back = out_strip
                        side = slice((parity + back) % 2 * C, ((parity + back) % 2 + 1) * C)
                        if strip:
                            pool.wait_ge(pool_h, 2 * (strip[0] * STRIPS + strip[1]) + 2)
                        else:
                            pool.wait_ge(pool_g, wb * STRIPS + w + 1)
                        pool.wait_ge(act_o, wb * STRIPS + w + 1)
                        nc.gpsimd.tensor_tensor(o[side, w % 2, :], o[side, w % 2, :],
                                                X[side, w * ROWS:(w + 1) * ROWS, :].rearrange("p r c -> p (r c)"),
                                                ALU.add).then_inc(pool_o, 1)
                    if dw:
                        bb, s, _ = dw
                        if out_strip:
                            pool.wait_ge(pool_o, wb * STRIPS + w + 1)
                        pool.wait_ge(act_g, bb * STRIPS + s + 1)
                        nc.gpsimd.tensor_tensor(g[:], g[:], gel[:], ALU.mult).then_inc(pool_g, 1)
                    if more and t == GROUP_STEP:
                        rstd_x(b + 1)
                    if more and t in NORM_STEPS:
                        pool.wait_ge(pool_g, bb * STRIPS + s + 1)
                        for j in NORM_STEPS[t]:
                            low_part(b + 1, 1 - parity, j)

            rstd_x(0)
            pool.wait_ge(pool_rstdx, 1)
            for j in range(STRIPS):
                low_part(0, 0, j)
            image(0, 0, False, True, True)
            with pool.Fori(0, (B - 2) // 2) as pair_of:
                image(pool.snap(pair_of * 2 + 1), 1, True, True, True)
                image(pool.snap(pair_of * 2 + 2), 0, True, True, True)
            image(B - 1, 1, True, True, False)
            image(B, 0, True, False, False)

        @block.scalar
        def _(act):
            def sum_strips(b, parity, todo, done):
                side = slice(parity * C, (parity + 1) * C)
                for k, (what, j) in enumerate(todo):
                    n = b * 2 * STRIPS + done + k
                    for part, (_, first, _) in enumerate(LOADS):
                        if j == first and what == 0:
                            act.wait_ge(dma_x[part], b * 16 + 16)
                    if (what, j) == (0, 0):
                        act.wait_ge(dve_bnx, b * 3 + 3)
                    if not isinstance(n, int) or n >= 2:
                        act.wait_ge(act_sum, n - 1)
                    nc.scalar.activation(junk[(done + k) % 2 * C:((done + k) % 2 + 1) * C],
                                         X[side, j * ROWS:(j + 1) * ROWS, :].rearrange("p a b -> p (a b)"),
                                         ACT.Square if what else ACT.Identity, scale=-1.0, bias=firstx[side, 0:1],
                                         accum_out=sums[side, what, j:j + 1]).then_inc(act_sum, 1)

            def groups_to_sbuf(b):
                act.wait_ge(pe_statx, b + 1)
                nc.scalar.copy(groupx[:], bank[6][:, 0:3]).then_inc(act_statx, 1)

            def normalise_strip(b, parity, j):
                side, other = (slice(q * C, (q + 1) * C) for q in (parity, 1 - parity))
                if j == 0:
                    act.wait_ge(dve_statx, b * 4 + 4)
                if j >= N32_BUFS:
                    act.wait_ge(pool_lo, b * STRIPS + j - N32_BUFS + 1)
                src = X[side, j * ROWS:(j + 1) * ROWS, :]
                for dst in (n32[side, j % N32_BUFS], S[other, 1 + j * ROWS:1 + (j + 1) * ROWS, 1:1 + W],
                            S[side, 1 + j * ROWS:1 + (j + 1) * ROWS, 1:1 + W]):
                    last = nc.scalar.activation(dst, src, ACT.Identity, bias=nbx[side], scale=rstdx[side])
                last.then_inc(act_hi, 1)

            def image(b, parity, prev, front, more):
                side = slice(parity * C, (parity + 1) * C)

                def normalise_x1(m):
                    if m == 0:
                        act.wait_ge(dve_stat1, b * 5 + 5)
                    if prev or m:
                        act.wait_ge(pe_xT, b * STRIPS + m)
                    nc.scalar.activation(xn[0:C].rearrange("p k r c -> p r k c"),
                                         X[side, m * ROWS:(m + 1) * ROWS, :].rearrange("p r (k c) -> p r k c", c=BW),
                                         ACT.Identity, bias=nb1[side], scale=rstd1[side]).then_inc(act_xn, 1)

                for t in range(STRIPS if front else OUT):
                    back_strip = item(b, t, BACK, prev, front)
                    out_strip = item(b, t, OUT, prev, front)
                    if front and t == 0:
                        normalise_x1(0)
                    if back_strip:
                        bb, i, back = back_strip
                        at = slot((parity + back) % 2, i)
                        row = at * ROWS
                        for half in range(2):
                            if half == 0:
                                if i >= 3:
                                    act.wait_ge(dve_tap, bb * TAPS_IMG + tap_base(i - 2, 0))
                                elif back or prev:
                                    act.wait_ge(dve_tap, (bb - 1) * TAPS_IMG + tap_base(i + STRIPS - 2, 0))
                            act.wait_ge(pe_h, 2 * (bb * STRIPS + i) + half + 1)
                            src = banks(4 + 2 * half, NBLK * BPX).rearrange("p (k r c) -> p k r c", k=NBLK, r=ROWS)
                            if at == 0:
                                nc.scalar.activation(h[:, half, RING + 1, 1:1 + W].rearrange("p (k c) -> p k c", c=BW),
                                                     src[:, :, 0, :], ACT.Copy)
                            if at == RING_STRIPS - 1:
                                nc.scalar.activation(h[:, half, 0, 1:1 + W].rearrange("p (k c) -> p k c", c=BW),
                                                     src[:, :, ROWS - 1, :], ACT.Copy)
                            nc.scalar.activation(
                                h[:, half, 1 + row:1 + row + ROWS, 1:1 + W].rearrange("p r (k c) -> p k r c", c=BW),
                                src, ACT.Copy).then_inc(act_h, 1)
                    dw = item(b, t, DW, prev, front)

                    def gated():
                        bb, s, _ = dw
                        act.wait_ge(dve_tap, bb * TAPS_IMG + tap_base(s, 1))
                        if s or prev:
                            act.wait_ge(pool_g, bb * STRIPS + s)
                        nc.scalar.activation(gel[:].rearrange("p (a b) -> p a b", a=2), PS[:, 0:2, 0:TILE],
                                             ACT.Gelu).then_inc(act_gel, 1)

                    if front:
                        n = t
                        act.wait_ge(pe_xT, b * STRIPS + n + 1)
                        if n or prev:
                            act.wait_ge(pe_xf, b * STRIPS + n)
                        nc.scalar.activation(xT[:], bank[4][:, 0:NBLK * C].rearrange("p (k c) -> p k c", c=C).unsqueeze(2)
                                             .broadcast_to([BPX, NBLK, 2, C]), ACT.Copy).then_inc(act_xT, 1)
                        if more and t == GROUP_STEP:
                            groups_to_sbuf(b + 1)
                    if dw:
                        gated()
                    if more and t in STAT_STEPS:
                        sums_before = sum(len(STAT_STEPS.get(u, ())) for u in range(t))
                        sum_strips(b + 1, 1 - parity, STAT_STEPS[t][:1], sums_before)
                    if front:
                        act.wait_ge(pe_xf, b * STRIPS + n + 1)
                        if n or prev:
                            act.wait_ge(pe_hf, 2 * (b * STRIPS + n))
                        spectrum = banks(6, NBLK * BPX).rearrange("p (k f) -> p k f", k=NBLK)
                        nc.scalar.activation(xf32[C:128], spectrum[C:128], ACT.Copy)
                        nc.scalar.activation(xf[:], spectrum, ACT.Copy).then_inc(act_xf, 1)
                    if out_strip:
                        wb, w, out_back = out_strip
                        side_out = slice((parity + out_back) % 2 * C, ((parity + out_back) % 2 + 1) * C)
                        act.wait_ge(pe_out, wb * STRIPS + w + 1)
                        if w >= 2 or prev:
                            act.wait_ge(dma_out[w % 2], 16 * (wb * (STRIPS // 2) + w // 2))
                        for q in range(2):
                            last = nc.scalar.activation(o[side_out, w % 2, q * TILE:(q + 1) * TILE],
                                                        bank[5][q * C:(q + 1) * C, 0:TILE], ACT.Copy)
                        last.then_inc(act_o, 1)
                    if dw:
                        bb, s, _ = dw
                        act.wait_ge(dve_tap, bb * TAPS_IMG + tap_base(s, 1) + TAP_OPS[s][1])
                        if s or prev:
                            act.wait_ge(pe_out, bb * STRIPS + s)
                        nc.scalar.activation(g[:].rearrange("p (a b) -> p a b", a=2), PS[:, 2:4, 0:TILE],
                                             ACT.Copy).then_inc(act_g, 1)
                    if back_strip:
                        bb, i, back = back_strip
                        for half in range(2):
                            act.wait_ge(act_h, 2 * (bb * STRIPS + i) + half + 1)
                            nc.scalar.activation(h16[:, 0, half, row:row + ROWS, 1:1 + W],
                                                 h[:, half, 1 + row:1 + row + ROWS, 1:1 + W],
                                                 ACT.Copy).then_inc(act_h16, 1)
                    if front and n + 1 < STRIPS:
                        normalise_x1(n + 1)
                    if more and t in STAT_STEPS:
                        sum_strips(b + 1, 1 - parity, STAT_STEPS[t][1:], sums_before + 1)
                    if more:
                        for j in NORM_STEPS.get(t, ()):
                            normalise_strip(b + 1, 1 - parity, j)

            sum_strips(0, 0, [(what, j) for what in range(2) for j in range(STRIPS)], 0)
            groups_to_sbuf(0)
            act.wait_ge(pool_zero, 8)
            for j in range(STRIPS):
                normalise_strip(0, 0, j)
            image(0, 0, False, True, True)
            with act.Fori(0, (B - 2) // 2) as pair_of:
                image(act.snap(pair_of * 2 + 1), 1, True, True, True)
                image(act.snap(pair_of * 2 + 2), 0, True, True, True)
            image(B - 1, 1, True, True, False)
            image(B, 0, True, False, False)

        @block.vector
        def _(dve):
            def first_strip_statx(b, parity):
                side = slice(parity * C, (parity + 1) * C)
                dve.wait_ge(dma_x[0], b * 16 + 16)
                for k in range(2):
                    nc.vector.bn_stats(bnx[side, k, :], X[side, k * HALF_ROWS:(k + 1) * HALF_ROWS, :]
                                       .rearrange("p a b -> p (a b)")).then_inc(dve_bnx, 1)
                dve.wait_ge(dve_bnx, b * 3 + 2)
                nc.vector.memset(offset[side], 0.0)
                nc.vector.bn_aggr(firstx[side], bnx[side].rearrange("p a b -> p (a b)")).then_inc(dve_bnx, 1)

            first_strip_statx(0, 0)
            dve.wait_ge(dma_conv, 48)
            nc.vector.tensor_scalar(cge[:], craw[:], 0.0, 2.0, ALU.is_ge, ALU.mult).then_inc(dve_sq, 1)
            dve.wait_ge(dve_sq, 1)
            dve.wait_ge(pool_zero, 8)
            for d in range(4):
                for odd in range(2):
                    ky = d - odd
                    if 0 <= ky < 3:
                        nc.vector.tensor_scalar(csign[:, d, :, odd * C:(odd + 1) * C], cge[:, 3 * ky:3 * ky + 3, :],
                                                1.0, None, ALU.subtract).then_inc(dve_csign, 1)
            dve.wait_ge(dma_const, 16 * N_CONST)
            nc.vector.tensor_copy(win_hi[:], win_sb[:]).then_inc(dve_sq, 1)
            nc.vector.tensor_copy(wdw_16[:], wdw_sb[:]).then_inc(dve_sq, 1)
            dve.wait_ge(dve_sq, 3)
            nc.vector.tensor_tensor(win_lo[:], win_sb[:], win_hi[:], ALU.subtract).then_inc(dve_prep, 1)
            nc.vector.tensor_copy(wdw_hi[:], wdw_16[:]).then_inc(dve_sq, 1)
            nc.vector.tensor_tensor(wdw_lo[:], wdw_sb[:], wdw_16[:], ALU.subtract).then_inc(dve_sq, 1)
            dve.wait_ge(dve_sq, 5)
            for half in range(2):
                for k, (dy, dx) in enumerate(PE_TAPS[half]):
                    at = (dy + 1) * 3 + dx + 1
                    nc.vector.tensor_scalar(diag_hi[:, half, k, :], c_id[:], wdw_hi[:, half, at:at + 1], None, ALU.mult)
                    nc.vector.tensor_scalar(diag_lo[:, half, k, :], c_id[:], wdw_lo[:, half, at:at + 1], None,
                                            ALU.mult).then_inc(dve_prep, 1)
            dve.wait_ge(pe_mult, 1)
            nc.vector.tensor_copy(mult[:], bank[5][:, 0:C2]).then_inc(dve_prep, 1)

            def channel_statx(b, parity):
                side = slice(parity * C, (parity + 1) * C)
                dve.wait_ge(act_sum, b * 2 * STRIPS + 2 * STRIPS)
                nc.vector.reduce_sum(totals[side], sums[side], axis=AX.X).then_inc(dve_sums, 1)
                dve.wait_ge(dve_sums, b * 3 + 1)
                nc.vector.scalar_tensor_tensor(out=mvx[side, 0:1], in0=totals[side, 0:1], scalar=-1.0 / IMG,
                                               in1=firstx[side, 0:1], op0=ALU.mult, op1=ALU.add)
                nc.vector.tensor_scalar(offset[side, 0:1], totals[side, 0:1], 1.0 / IMG, None,
                                        ALU.mult).then_inc(dve_sums, 1)
                dve.wait_ge(dve_sums, b * 3 + 2)
                nc.vector.tensor_tensor(offset[side, 1:2], offset[side, 0:1], offset[side, 0:1],
                                        ALU.mult).then_inc(dve_sums, 1)
                dve.wait_ge(dve_sums, b * 3 + 3)
                nc.vector.scalar_tensor_tensor(out=mvx[side, 1:2], in0=totals[side, 1:2], scalar=1.0 / IMG,
                                               in1=offset[side, 1:2], op0=ALU.mult, op1=ALU.subtract).then_inc(dve_statx, 1)

            def group_statx(b):
                dve.wait_ge(act_statx, b + 1)
                nc.vector.scalar_tensor_tensor(out=varx[:], in0=groupx[:, 2:3], scalar=groupx[:, 2:3],
                                               in1=groupx[:, 1:2], op0=ALU.mult, op1=ALU.add).then_inc(dve_statx, 1)
                dve.wait_ge(dve_statx, b * 4 + 2)
                nc.vector.tensor_scalar(vex[:], varx[:], 0.0, GN_EPS, ALU.max, ALU.add).then_inc(dve_statx, 1)

            def shift_x(b):
                dve.wait_ge(pool_rstdx, b + 1)
                nc.vector.scalar_tensor_tensor(out=nbx[:], in0=groupx[:, 0:1], scalar=-1.0, in1=rstdx[:],
                                               op0=ALU.mult, op1=ALU.mult).then_inc(dve_statx, 1)

            def taps(bb, parity, s, half, which):
                base = bb * TAPS_IMG + tap_base(s, half)
                k = 0
                for n, (dy, dx) in enumerate(DVE_TAPS[half]):
                    at = (dy + 1) * 3 + dx + 1
                    for i0, i1 in tap_pieces(s, dy):
                        k += 1
                        if n not in which:
                            continue
                        if k > 1:
                            dve.wait_ge(dve_tap, base + k - 1)
                        elif half == 0:
                            dve.wait_ge(pe_dwA, bb * STRIPS + s + 1)
                        else:
                            dve.wait_ge(pe_dwB, bb * STRIPS + s + 1)
                        if dy == 1 and s + 1 < STRIPS and DVE_TAPS[half][n - 1][0] != 1:
                            dve.wait_ge(act_h, 2 * (bb * STRIPS + s + 1) + half + 1)
                        row = 1 + slot(parity, s) * ROWS + i0 + dy
                        src = h[:, half, row:row + i1 - i0, 1 + dx:1 + dx + W]
                        if i1 - i0 == ROWS:
                            acc = PS[:, 2 * half:2 * half + 2, 0:TILE].rearrange("p a (r c) -> p a r c", c=W)
                            src = src.rearrange("p (a r) c -> p a r c", a=2)
                        else:
                            q = i0 // HALF_ROWS
                            acc = bank[2 * half + q][:, (i0 - q * HALF_ROWS) * W:(i1 - q * HALF_ROWS) * W]
                            acc = acc.rearrange("p (r c) -> p r c", c=W)
                        nc.vector.scalar_tensor_tensor(out=acc, in0=src, scalar=wdw_sb[:, half, at:at + 1], in1=acc,
                                                       op0=ALU.mult, op1=ALU.add).then_inc(dve_tap, 1)

            def convolved(b, parity, strips):
                side = slice(parity * C, (parity + 1) * C)

                def evacuate(pos, j):
                    dve.wait_ge(pe_conv, b * STRIPS + j + 1)
                    for odd in range(2):
                        rows = slice(j * ROWS + odd, (j + 1) * ROWS, 2)
                        nc.vector.scalar_tensor_tensor(
                            out=X[side, rows, :],
                            in0=bank[conv_bank(strips, pos)][odd * C:(odd + 1) * C, 0:TILE].rearrange("p (r c) -> p r c", c=W),
                            scalar=alpha_sb[odd * C:(odd + 1) * C], in1=X[side, rows, :],
                            op0=ALU.mult, op1=ALU.add).then_inc(dve_conv, 1)

                def statistics(j):
                    dve.wait_ge(dve_conv, 2 * (b * STRIPS + j) + 2)
                    for k in range(2):
                        row0 = j * ROWS + k * HALF_ROWS
                        nc.vector.bn_stats(bn[side, 2 * j + k, :],
                                           X[side, row0:row0 + HALF_ROWS, :].rearrange("p a b -> p (a b)")).then_inc(dve_bn, 1)

                ahead = 2 if len(strips) > 2 else 1
                for first in range(0, len(strips), 3):
                    group = range(first, min(first + 3, len(strips)))
                    for pos in group[:ahead]:
                        evacuate(pos, strips[pos])
                    for pos in group:
                        if pos >= first + ahead:
                            evacuate(pos, strips[pos])
                        statistics(strips[pos])
                if strips[-1] == STRIPS - 1:
                    other = slice((1 - parity) * C, (2 - parity) * C)
                    dve.wait_ge(dve_bn, 2 * (b * STRIPS + STRIPS))
                    nc.vector.memset(mv[other], 0.0)
                    nc.vector.bn_aggr(mv[side], bn[side].rearrange("p a b -> p (a b)")).then_inc(dve_stat1, 1)

            def group_stat1(b):
                dve.wait_ge(pe_stat1, b + 1)
                nc.vector.tensor_copy(group1[:], bank[2][:, 0:3]).then_inc(dve_stat1, 1)
                dve.wait_ge(dve_stat1, b * 5 + 2)
                nc.vector.scalar_tensor_tensor(out=var1[:], in0=group1[:, 2:3], scalar=group1[:, 2:3],
                                               in1=group1[:, 1:2], op0=ALU.mult, op1=ALU.add).then_inc(dve_stat1, 1)
                dve.wait_ge(dve_stat1, b * 5 + 3)
                nc.vector.tensor_scalar(ve1[:], var1[:], GN_EPS, None, ALU.add).then_inc(dve_stat1, 1)

            def image(b, parity, prev, front, more):
                side = slice(parity * C, (parity + 1) * C)
                for t in range(STRIPS if front else OUT):
                    dw = item(b, t, DW, prev, front)
                    back_strip = item(b, t, BACK, prev, front)
                    if dw:
                        bb, s, back = dw
                        par = (parity + back) % 2
                        taps(bb, par, s, 0, range(0, 1))
                    if more and t == GROUP_STEP + 1:
                        group_statx(b + 1)
                    if t == 0 and front:
                        group_stat1(b)
                    if dw:
                        taps(bb, par, s, 0, range(1, HF_AFTER))
                    if t == 0 and front:
                        dve.wait_ge(pool_rstd1, b + 1)
                        nc.vector.scalar_tensor_tensor(out=nb1[:], in0=group1[:, 0:1], scalar=-1.0, in1=rstd1[:],
                                                       op0=ALU.mult, op1=ALU.mult).then_inc(dve_stat1, 1)
                    if back_strip:
                        fb, i, _ = back_strip
                        if i or back_strip[2] or prev:
                            dve.wait_ge(pe_h, 2 * (fb * STRIPS + i))
                        for part, (at, k0, k1) in enumerate(((6, 0, 4), (4, 4, NBLK))):
                            dve.wait_ge(pe_hf, 2 * (fb * STRIPS + i) + part + 1)
                            nc.vector.tensor_tensor(
                                hf[:, k0:k1, :], banks(at, (k1 - k0) * C2).rearrange("p (k c) -> p k c", c=C2),
                                mult[:].unsqueeze(1).broadcast_to([BPX, k1 - k0, C2]), ALU.mult).then_inc(dve_hf, 1)
                    if more and t == min(STAT_STEPS):
                        first_strip_statx(b + 1, 1 - parity)
                    if dw:
                        taps(bb, par, s, 0, range(HF_AFTER, 9))
                    if more and t == GROUP_STEP:
                        channel_statx(b + 1, 1 - parity)
                    if dw:
                        taps(bb, par, s, 1, range(9))
                    if more and t == GROUP_STEP + 1:
                        shift_x(b + 1)
                    if more and t in CONV_STEPS:
                        convolved(b + 1, 1 - parity, CONV_STEPS[t])

            channel_statx(0, 0)
            group_statx(0)
            shift_x(0)
            convolved(0, 0, range(STRIPS))
            image(0, 0, False, True, True)
            with dve.Fori(0, (B - 2) // 2) as pair_of:
                image(dve.snap(pair_of * 2 + 1), 1, True, True, True)
                image(dve.snap(pair_of * 2 + 2), 0, True, True, True)
            image(B - 1, 1, True, True, False)
            image(B, 0, True, False, False)

        @block.tensor
        def _(pe):
            def groups(into, channels):
                nc.tensor.matmul(into[:, 0:2], c_pair[:], channels[:], start=True, stop=True)
                return nc.tensor.matmul(into[:, 2:3], c_apart[:], channels[:, 0:1], start=True, stop=True)

            def groups_x(b):
                pe.wait_ge(dve_statx, b * 4 + 1)
                groups(bank[6], mvx).then_inc(pe_statx, 1)

            def convolution(b, strips, banks01=None, bank7=None):
                for pos, j in enumerate(strips):
                    pe.wait_ge(pool_lo, b * STRIPS + min(j + 2, STRIPS))
                    if pos >= 3:
                        pe.wait_ge(dve_conv, 2 * (b * STRIPS + j - 2))
                    if pos == 0 and banks01:
                        pe.wait_ge(*banks01)
                    if conv_bank(strips, pos) == 7 and bank7:
                        pe.wait_ge(*bank7)
                    for d in range(4):
                        for kx in range(3):
                            row0 = j * ROWS + d
                            last = nc.tensor.matmul(bank[conv_bank(strips, pos)][:, 0:TILE], csign[:, d, kx, :],
                                                    S[:, row0:row0 + ROWS - 1:2, kx:kx + W],
                                                    start=(d == 0 and kx == 0), stop=(d == 3 and kx == 2))
                    last.then_inc(pe_conv, 1)

            def depthwise(parity, s, half):
                for q in range(2):
                    todo = []
                    for k, (dy, dx) in enumerate(PE_TAPS[half]):
                        rows = [i for i in range(q * HALF_ROWS, (q + 1) * HALF_ROWS) if 0 <= s * ROWS + i + dy < H]
                        first = (slot(parity, s) * ROWS + rows[0] + dy) % RING
                        cut = min(len(rows), RING - first)
                        for i0, n, row in ((rows[0], cut, first), (rows[0] + cut, len(rows) - cut, 0)):
                            if n > 0:
                                at = (i0 - q * HALF_ROWS) * W
                                for data, weights in ((0, diag_hi), (1, diag_hi), (0, diag_lo)):
                                    todo.append((bank[2 * half + q][:, at:at + n * W], weights[:, half, k, :],
                                                 h16[:, data, half, row:row + n, 1 + dx:1 + dx + W]))
                    for m, (acc, weights, rows) in enumerate(todo):
                        last = nc.tensor.matmul(acc, weights, rows, start=(m == 0), stop=(m == len(todo) - 1),
                                                skip_group_check=True)
                return last

            pe.wait_ge(dma_const, 16 * N_CONST)
            nc.tensor.matmul(bank[5][:, 0:C2], c_pick[:], filt_sb[:], start=True, stop=True).then_inc(pe_mult, 1)
            pe.wait_ge(pool_zero, 8)
            groups_x(0)
            pe.wait_ge(dve_csign, 6)
            pe.wait_ge(act_statx, 1)
            convolution(0, range(STRIPS))
            pe.wait_ge(dve_prep, sum(map(len, PE_TAPS)) + 2)

            def image(b, parity, prev, front, more):
                for t in range(STRIPS if front else OUT):
                    back_strip = item(b, t, BACK, prev, front)
                    dw = item(b, t, DW, prev, front)
                    out_strip = item(b, t, OUT, prev, front)
                    conv_done = [None, None]
                    if (t == 0 and front and prev) or (more and t - 1 in CONV_STEPS):
                        conv_image, strips = (b, CONV_STEPS[STRIPS - 1]) if t == 0 else (b + 1, CONV_STEPS[t - 1])
                        last01 = [j for pos, j in enumerate(strips) if conv_bank(strips, pos) != 7][-1]
                        conv_done = [2 * (conv_image * STRIPS + j + 1) for j in (last01, strips[-1])]
                    if dw:
                        bb, s, back = dw
                        pe.wait_ge(pool_h, 2 * (bb * STRIPS + s) + 2)
                        if conv_done[0] is not None:
                            pe.wait_ge(dve_conv, conv_done[0])
                        if s or prev:
                            pe.wait_ge(act_gel, bb * STRIPS + s)
                        depthwise((parity + back) % 2, s, 0).then_inc(pe_dwA, 1)
                    if t == 0 and front:
                        pe.wait_ge(dve_stat1, b * 5 + 1)
                        if prev:
                            pe.wait_ge(act_g, bb * STRIPS + s)
                        groups(bank[2], mv).then_inc(pe_stat1, 1)
                    if back_strip:
                        bb, i, _ = back_strip
                        pe.wait_ge(pool_xf, bb * STRIPS + i + 1)
                        if conv_done[1] is not None:
                            pe.wait_ge(dve_conv, conv_done[1])
                        for at, k0, k1 in ((6, 0, 4), (4, 4, NBLK)):
                            if at == 4 and (t > OUT or prev):
                                pe.wait_ge(act_o, b * STRIPS + t - OUT)
                            for k in range(k0, k1):
                                for weights in (win_hi, win_lo):
                                    last = nc.tensor.matmul(banks(at, (k1 - k0) * C2)[:, (k - k0) * C2:(k - k0 + 1) * C2],
                                                            xf[:, k, :], weights[:], start=weights is win_hi,
                                                            stop=weights is win_lo)
                            last.then_inc(pe_hf, 1)
                    if t == 0 and front:
                        pe.wait_ge(dve_stat1, b * 5 + 2)
                    if dw:
                        bb, s, back = dw
                        if s or prev:
                            pe.wait_ge(act_g, bb * STRIPS + s)
                        depthwise((parity + back) % 2, s, 1).then_inc(pe_dwB, 1)
                    if back_strip:
                        bb, i, _ = back_strip
                        pe.wait_ge(dve_hf, 2 * (bb * STRIPS + i) + 2)
                        for half in range(2):
                            for k in range(NBLK):
                                last = nc.tensor.matmul(banks(4 + 2 * half, NBLK * BPX)[:, k * BPX:(k + 1) * BPX],
                                                        hf[:, k, half * HC:(half + 1) * HC], c_inv[:],
                                                        start=True, stop=True)
                            last.then_inc(pe_h, 1)

                    def transposed():
                        if back_strip:
                            pe.wait_ge(act_h, 2 * (back_strip[0] * STRIPS + back_strip[1]) + 1)
                        pe.wait_ge(act_xn, b * STRIPS + t + 1)
                        nc.tensor.transpose(bank[4][:, (NBLK - 1) * C:(NBLK + 1) * C],
                                            xn[:, NBLK - 1].rearrange("p r c -> p (r c)"), c_id[:])
                        for k in range(NBLK - 1):
                            last = nc.tensor.transpose(bank[4][:, k * C:(k + 1) * C],
                                                       xn[0:C, k].rearrange("p r c -> p (r c)"), c_id[0:C, 0:C])
                        last.then_inc(pe_xT, 1)

                    if front:
                        transposed()
                    if out_strip:
                        bb, w, _ = out_strip
                        pe.wait_ge(pool_g, bb * STRIPS + w + 1)
                        if back_strip:
                            pe.wait_ge(act_h, 2 * (back_strip[0] * STRIPS + back_strip[1]) + 1)
                        elif w:
                            pe.wait_ge(act_o, bb * STRIPS + w)
                        for q in range(2):
                            last = nc.tensor.matmul(bank[5][q * C:(q + 1) * C, 0:TILE], wout_sb[:],
                                                    g[:, q * TILE:(q + 1) * TILE], start=True, stop=True)
                        last.then_inc(pe_out, 1)
                    if front:
                        if back_strip:
                            pe.wait_ge(act_h, 2 * (back_strip[0] * STRIPS + back_strip[1]) + 2)
                        if more and t == GROUP_STEP:
                            groups_x(b + 1)
                            pe.wait_ge(act_statx, b + 2)
                        pe.wait_ge(act_xT, b * STRIPS + t + 1)
                        for k in range(NBLK):
                            last = nc.tensor.matmul(banks(6, NBLK * BPX)[:, k * BPX:(k + 1) * BPX],
                                                    xT[:, k].rearrange("p a c -> p (a c)"), c_fwd[:], start=True, stop=True)
                        last.then_inc(pe_xf, 1)
                    if more and t in CONV_STEPS:
                        convolution(b + 1, CONV_STEPS[t],
                                    banks01=(act_gel, dw[0] * STRIPS + dw[1] + 1),
                                    bank7=(act_xf, b * STRIPS + t + 1))

            image(0, 0, False, True, True)
            with pe.Fori(0, (B - 2) // 2) as pair_of:
                image(pe.snap(pair_of * 2 + 1), 1, True, True, True)
                image(pe.snap(pair_of * 2 + 2), 0, True, True, True)
            image(B - 1, 1, True, True, False)
            image(B, 0, True, False, False)


def kernel(x, L0_conv_weight, L0_conv_alpha, L1_conv_w_in, L1_conv_w_dw, L1_conv_fft_filt, L1_conv_w_out):
    import concourse.bacc as bacc
    from concourse.bass_utils import run_bass_kernel_spmd

    nc = bacc.Bacc("TRN2", target_bir_lowering=False, num_devices=1)
    nc.disable_value_cache = True
    arrays = {
        "x": np.ascontiguousarray(x),
        "conv_w": np.ascontiguousarray(np.transpose(np.asarray(L0_conv_weight), (1, 2, 3, 0))).reshape(C, 9, C),
        "alpha": np.ascontiguousarray(L0_conv_alpha).reshape(C, 1),
        "w_in": np.ascontiguousarray(np.transpose(np.asarray(L1_conv_w_in))),
        "w_dw": np.ascontiguousarray(L1_conv_w_dw).reshape(C2, 9),
        "filt": np.ascontiguousarray(np.transpose(np.asarray(L1_conv_fft_filt).reshape(C2, P * (P // 2 + 1)))),
        "w_out": np.ascontiguousarray(np.transpose(np.asarray(L1_conv_w_out))),
    }
    for name, a in shape_constants().items():
        arrays[name] = np.ascontiguousarray(a, dtype=np.float32)
    aps = {name: nc.dram_tensor(f"in_{name}", a.shape, F32, kind="ExternalInput").ap() for name, a in arrays.items()}
    out = nc.dram_tensor("out_x", arrays["x"].shape, F32, kind="ExternalOutput").ap()
    build(nc, *aps.values(), out)
    ran = run_bass_kernel_spmd(nc, [{f"in_{name}": a for name, a in arrays.items()}], core_ids=[0])
    return ran.results[0]["out_x"]
```
